# Optimizing a Trainium2 kernel written in Bass

```python
import numpy as np
import jax
import jax.numpy as jnp

def _softmax(x, axis=-1):
    return jax.nn.softmax(x, axis=axis)

def _gelu(x):
    return jax.nn.gelu(x, approximate=True)

def _silu(x):
    return jax.nn.silu(x)

def _sigmoid(x):
    return jax.nn.sigmoid(x)

def _layernorm(x, axis=-1, eps=1e-05):
    m = jnp.mean(x, axis=axis, keepdims=True)
    v = jnp.var(x, axis=axis, keepdims=True)
    return (x - m) / jnp.sqrt(v + eps)

def _scatter_add(tgt, idx, src, axis=0):
    return tgt.at[idx].add(src)

def _segment_sum(src, seg, n):
    return jax.ops.segment_sum(src, seg, n)
kernel_name = 'mk_prb_d1_jaxref_r8_f0496d'

def setup_inputs(seed: int=0):
    np.random.seed(seed)
    _w = jnp.asarray

    def _L0_attn_setup():
        import jax, jax.numpy as jnp
        import numpy as np
        import math
        NUM_HEADS = 16

        def get_slopes(n):

            def pow2(n):
                start = 2 ** (-2 ** (-(math.log2(n) - 3)))
                return [start * start ** i for i in range(n)]
            if math.log2(n).is_integer():
                return pow2(n)
            c = 2 ** math.floor(math.log2(n))
            return pow2(c) + get_slopes(2 * c)[0::2][:n - c]
        key = jax.random.key(seed)
        ks = jax.random.split(key, 5)
        B, T, C = (2, 256, 128)
        return {'x': jax.random.normal(ks[0], (B, T, C), dtype=jnp.float32), 'W_qkv': jax.random.normal(ks[1], (C, 3 * C), dtype=jnp.float32) * 0.02, 'b_qkv': jax.random.normal(ks[2], (3 * C,), dtype=jnp.float32) * 0.02, 'W_proj': jax.random.normal(ks[3], (C, C), dtype=jnp.float32) * 0.02, 'b_proj': jax.random.normal(ks[4], (C,), dtype=jnp.float32) * 0.02}
    _L0_attn_in = _L0_attn_setup()

    def _L0_ffn_setup():
        import jax, jax.numpy as jnp
        import numpy as np
        B, S, D_MODEL, D_FF, E, R, TOP_K = (4, 256, 128, 512, 8, 16, 2)
        key = jax.random.key(seed)
        ks = jax.random.split(key, 9)
        sd = 1.0 / np.sqrt(D_MODEL)
        return {'hidden_states': jax.random.normal(ks[0], (B, S, D_MODEL), jnp.float32), 'wi': jax.random.normal(ks[1], (D_FF, D_MODEL), jnp.float32) * sd, 'bi': jax.random.normal(ks[2], (D_FF,), jnp.float32) * 0.01, 'wo': jax.random.normal(ks[3], (D_MODEL, D_FF), jnp.float32) * (1.0 / np.sqrt(D_FF)), 'bo': jax.random.normal(ks[4], (D_MODEL,), jnp.float32) * 0.01, 'lora_A': jax.random.normal(ks[5], (E, R, D_MODEL), jnp.float32) * sd, 'lora_B': jax.random.normal(ks[6], (E, D_FF, R), jnp.float32) * 0.02, 'gate_w': jax.random.normal(ks[7], (E, D_MODEL), jnp.float32) * sd, 'gate_b': jax.random.normal(ks[8], (E,), jnp.float32) * 0.01}
    _L0_ffn_in = _L0_ffn_setup()
    _d = {'L0_attn_x': _L0_attn_in['x'], 'L0_attn_W_qkv': _L0_attn_in['W_qkv'], 'L0_attn_b_qkv': _L0_attn_in['b_qkv'], 'L0_attn_W_proj': _L0_attn_in['W_proj'], 'L0_attn_b_proj': _L0_attn_in['b_proj'], 'L0_ffn_wi': _L0_ffn_in['wi'], 'L0_ffn_bi': _L0_ffn_in['bi'], 'L0_ffn_wo': _L0_ffn_in['wo'], 'L0_ffn_bo': _L0_ffn_in['bo'], 'L0_ffn_lora_A': _L0_ffn_in['lora_A'], 'L0_ffn_lora_B': _L0_ffn_in['lora_B'], 'L0_ffn_gate_w': _L0_ffn_in['gate_w'], 'L0_ffn_gate_b': _L0_ffn_in['gate_b']}
    _x0 = _d['L0_attn_x']
    _d['L0_attn_x'] = jax.random.normal(jax.random.fold_in(jax.random.key(seed), 1), (4, 1024, 128), dtype=_x0.dtype)
    del _x0
    return _d

def reference(L0_attn_x, L0_attn_W_qkv, L0_attn_b_qkv, L0_attn_W_proj, L0_attn_b_proj, L0_ffn_wi, L0_ffn_bi, L0_ffn_wo, L0_ffn_bo, L0_ffn_lora_A, L0_ffn_lora_B, L0_ffn_gate_w, L0_ffn_gate_b):

    def _L0_attn_ref(x, W_qkv, b_qkv, W_proj, b_proj):
        import jax, jax.numpy as jnp
        import numpy as np
        import math
        NUM_HEADS = 16

        def get_slopes(n):

            def pow2(n):
                start = 2 ** (-2 ** (-(math.log2(n) - 3)))
                return [start * start ** i for i in range(n)]
            if math.log2(n).is_integer():
                return pow2(n)
            c = 2 ** math.floor(math.log2(n))
            return pow2(c) + get_slopes(2 * c)[0::2][:n - c]
        B, T, C = x.shape
        H = NUM_HEADS
        D = C // H
        qkv = x @ W_qkv + b_qkv
        q, k, v = jnp.split(qkv, 3, axis=-1)
        q = q.reshape(B, T, H, D).transpose(0, 2, 1, 3)
        k = k.reshape(B, T, H, D).transpose(0, 2, 1, 3)
        v = v.reshape(B, T, H, D).transpose(0, 2, 1, 3)
        slopes = jnp.asarray(get_slopes(H), dtype=jnp.float32)
        idx = jnp.arange(T)
        alibi = jnp.minimum(idx[None, :] - idx[:, None], 0).astype(jnp.float32)
        bias = slopes[:, None, None] * alibi
        scale = 1.0 / math.sqrt(D)
        scores = jnp.einsum('bhtd,bhsd->bhts', q, k) * scale + bias[None]
        w = jax.nn.softmax(scores, axis=-1)
        y = jnp.einsum('bhts,bhsd->bhtd', w, v)
        y = y.transpose(0, 2, 1, 3).reshape(B, T, C)
        return y @ W_proj + b_proj

    def _L0_ffn_ref(hidden_states, wi, bi, wo, bo, lora_A, lora_B, gate_w, gate_b):
        import jax, jax.numpy as jnp
        import numpy as np
        B, S, D_MODEL, D_FF, E, R, TOP_K = (4, 256, 128, 512, 8, 16, 2)
        logits = jnp.einsum('bsd,ed->bse', hidden_states, gate_w) + gate_b
        scores = jax.nn.softmax(logits, axis=-1)
        top_v, top_i = jax.lax.top_k(scores, TOP_K)
        val_sum = top_v.sum(axis=-1)
        out = jnp.zeros_like(hidden_states)
        for e in range(E):
            count = (top_i == e).sum(axis=-1).astype(hidden_states.dtype)
            gate = count * val_sum
            inter = jnp.einsum('bsd,fd->bsf', hidden_states, wi) + bi + jnp.einsum('bsr,fr->bsf', jnp.einsum('bsd,rd->bsr', hidden_states, lora_A[e]), lora_B[e])
            h = jax.nn.relu(inter)
            expert_out = jnp.einsum('bsf,df->bsd', h, wo) + bo
            out = out + gate[..., None] * expert_out
        return out
    x = L0_attn_x
    xn = _layernorm(x, axis=-1)
    x = x + _L0_attn_ref(xn, L0_attn_W_qkv, L0_attn_b_qkv, L0_attn_W_proj, L0_attn_b_proj) + _L0_ffn_ref(xn, L0_ffn_wi, L0_ffn_bi, L0_ffn_wo, L0_ffn_bo, L0_ffn_lora_A, L0_ffn_lora_B, L0_ffn_gate_w, L0_ffn_gate_b)
    return x

_drawn_inputs = setup_inputs


def setup_inputs(seed=0):
    import zlib

    import numpy as np

    out = dict(_drawn_inputs(seed))
    spreads = {}
    factors = {'L0_attn_W_qkv': 8.0,
     'L0_attn_b_qkv': 8.0,
     'L0_attn_W_proj': 8.0,
     'L0_attn_b_proj': 3.608,
     'L0_ffn_bi': 8.0,
     'L0_ffn_bo': 6.361,
     'L0_ffn_gate_b': 26.795}
    for name, (base, spread) in spreads.items():
        noise = np.random.default_rng([zlib.crc32(name.encode()), seed]).standard_normal(out[name].shape)
        drawn = base * np.exp(spread * noise) if base else spread * noise
        out[name] = jnp.asarray(drawn.astype(out[name].dtype))
    for name, factor in factors.items():
        out[name] = (out[name] * factor).astype(out[name].dtype)
    return out
```

```python
from contextlib import ExitStack

import numpy as np

import concourse.bass as bass
from concourse import mybir

F32 = mybir.dt.float32
BF16 = mybir.dt.bfloat16
ALU = mybir.AluOpType
ACT = mybir.ActivationFunctionType
AX_X = mybir.AxisListType.X

P = 128
B, T, C, H, D = 4, 1024, 128, 16, 8
E, R, F = 8, 16, 512
NT = T // P
TILES = B * NT
CT = 4
CHUNK = CT * P
CHUNKS = TILES // CT
PAIRS = H // 2
UNITS = B * PAIRS
COMBOS_Q = (0, 0, 1, 1, 0, 2)
COMBOS_K = (0, 1, 0, 1, 2, 0)
NC = len(COMBOS_Q)
QK = NC * D
MX = 3
MAIN = QK + MX
BR = 12
ALL = 2 * (MAIN + BR)
STEP = 32
RING = 3
VP = 32
EPS = 1e-5
SCALE = 1.0 / float(np.sqrt(D))
BV, BP, BO, GB = 0, C, 2 * C, 3 * C
BQ, BK, BI = 0, 1, 2
XV, XA, XG = 0, C, 2 * C
XW = 2 * C + E


def wait(eng, sem, value):
    if isinstance(value, int) and value <= 0:
        return
    eng.wait_ge(sem, value)


def chunks(body, eng, ends=1):
    for c in range(ends):
        body(c, c % 2)
    with eng.Fori(0, CHUNKS // 2 - ends) as t:
        for k in range(ends, ends + 2):
            body(t * 2 + k, k % 2)
    for c in range(CHUNKS - ends, CHUNKS):
        body(c, c % 2)


def build(nc, x, w_q, w_k, w_x, w_i, w_b, w_o, w_p, bias_rows, bias_cols, ident_in, iota_in,
          q_rows, k_rows, const_rows, factors, out):
    with ExitStack() as ctx:
        def sb(name, shape, dt=F32):
            return ctx.enter_context(nc.sbuf_tensor(name, shape, dt))

        def sem(name):
            return ctx.enter_context(nc.semaphore(name))

        q_parts = nc.dram_tensor("q_parts", (UNITS, 2, NC, D, T), BF16, kind="Internal").ap()
        k_parts = nc.dram_tensor("k_parts", (UNITS, 2, NC, D, T), BF16, kind="Internal").ap()

        acc = sb("acc", [P, TILES, C])
        values = sb("values", [P, UNITS, NT, 2, D])
        heads_out = sb("heads_out", [P, UNITS, NT, 2 * D])
        brow = sb("brow", [P, 3 * C + E])
        bcol = sb("bcol", [P, 6])
        ident = sb("ident", [P, P])
        ident_b = sb("ident_b", [P, P], BF16)
        wp = sb("wp", [P, C])

        k_stage = sb("k_stage", [P, RING, 2, 2, T], BF16)

        psum = ctx.enter_context(nc.psum_tensor("psum", [P, 8, 512], F32))

        with ExitStack() as ph:
            def tmp(name, shape, dt=F32):
                return ph.enter_context(nc.sbuf_tensor(name, shape, dt))

            xc = tmp("xc", [P, TILES, C])
            wq = tmp("wq", [P, C])
            wk = tmp("wk", [P, C])
            wx = tmp("wx", [P, XW])
            wi = tmp("wi", [P, F])
            wb = tmp("wb", [P, F])
            wo = tmp("wo", [P, F // P, C])
            iota = tmp("iota", [P, CT, E])
            bqs = tmp("bqs", [P, 1])
            rstd = tmp("rstd", [P, TILES])
            bo2 = tmp("bo2", [P, C])
            sums = tmp("sums", [P, TILES])
            mean = tmp("mean", [P, TILES])
            ssq = tmp("ssq", [P, TILES])
            junk = tmp("junk", [P, TILES, C])
            var = tmp("var", [P, TILES])
            root = tmp("root", [P, TILES])
            rinv = tmp("rinv", [P, TILES])
            quo = tmp("quo", [P, TILES])
            root2 = tmp("root2", [P, TILES])

            s_x = [sem(f"x_loaded{b}") for b in range(B)]
            s_w = sem("weights_loaded")
            s_sum = sem("row_sums")
            s_mean = sem("means")
            s_xc = sem("centred")
            s_ssq = sem("squares_summed")
            s_chain = sem("variance_chain")
            s_root = sem("rooted")
            s_const = sem("constants_made")
            k_blank = sem("k_stage_blank")
            W_LOADS = 11
            with nc.Block() as block:
                x_v = x.rearrange("b (n p) d -> b p n d", p=P)

                @block.sync
                def _(sp):
                    for b in range(B):
                        sp.dma_start(acc[:, b * NT:(b + 1) * NT, :], x_v[b]).then_inc(s_x[b], 16)
                    for dst, src in ((wq, w_q), (wk, w_k), (wx, w_x), (wi, w_i), (wb, w_b), (wp, w_p),
                                     (brow, bias_rows), (bcol, bias_cols), (ident, ident_in)):
                        sp.dma_start(dst[:, :], src).then_inc(s_w, 16)
                    sp.dma_start(wo[:, :, :], w_o).then_inc(s_w, 16)
                    sp.dma_start(iota[:, :, :], iota_in).then_inc(s_w, 16)

                @block.gpsimd
                def _(pool):
                    nc.gpsimd.memset(k_stage[:, :, :, :, :], 0.0).then_inc(k_blank, 1)

                @block.vector
                def _(dve):
                    for b in range(B):
                        g = slice(b * NT, (b + 1) * NT)
                        dve.wait_ge(s_x[b], 16)
                        nc.vector.tensor_reduce(sums[:, g], acc[:, g, :], AX_X, ALU.add).then_inc(s_sum, 1)
                        dve.wait_ge(s_sum, b + 1)
                        nc.vector.tensor_scalar(mean[:, g], sums[:, g], 1.0 / C, None, ALU.mult).then_inc(s_mean, 1)
                        dve.wait_ge(s_mean, b + 1)
                        nc.vector.tensor_tensor(
                            xc[:, g, :], acc[:, g, :], mean[:, g].unsqueeze(2).to_broadcast([P, NT, C]),
                            ALU.subtract).then_inc(s_xc, 1)
                    dve.wait_ge(s_ssq, TILES)
                    nc.vector.tensor_scalar(var[:, :], ssq[:, :], 1.0 / C, EPS, ALU.mult, ALU.add).then_inc(s_chain, 1)
                    dve.wait_ge(s_root, 1)
                    nc.vector.reciprocal(rinv[:, :], root[:, :]).then_inc(s_chain, 1)
                    dve.wait_ge(s_chain, 2)
                    nc.vector.tensor_tensor(quo[:, :], var[:, :], rinv[:, :], ALU.mult).then_inc(s_chain, 1)
                    dve.wait_ge(s_chain, 3)
                    nc.vector.tensor_tensor(sums[:, :], quo[:, :], root[:, :], ALU.add).then_inc(s_chain, 1)
                    dve.wait_ge(s_chain, 4)
                    nc.vector.tensor_scalar(root2[:, :], sums[:, :], 0.5, None, ALU.mult).then_inc(s_chain, 1)
                    dve.wait_ge(s_chain, 5)
                    nc.vector.reciprocal(rstd[:, :], root2[:, :]).then_inc(s_chain, 1)
                    dve.wait_ge(s_w, 16 * W_LOADS)
                    nc.vector.tensor_copy(ident_b[:, :], ident[:, :]).then_inc(s_const, 1)
                    nc.vector.tensor_scalar(bqs[:, :], bcol[:, BQ:BQ + 1], SCALE, None, ALU.mult).then_inc(s_const, 1)
                    nc.vector.tensor_scalar(bo2[:, :], brow[:, BO:BO + C], 2.0, None, ALU.mult).then_inc(s_const, 1)

                @block.scalar
                def _(act):
                    for n in range(TILES):
                        act.wait_ge(s_xc, n // NT + 1)
                        nc.scalar.activation(junk[:, n, :], xc[:, n, :], ACT.Square,
                                             accum_out=ssq[:, n:n + 1]).then_inc(s_ssq, 1)
                    act.wait_ge(s_chain, 1)
                    nc.scalar.activation(root[:, :], var[:, :], ACT.Sqrt).then_inc(s_root, 1)

            phase1(nc, ph, sem, psum, acc, values, brow, bcol, ident, xc, wq, wk, wx, wi, wb, wo, iota,
                   bqs, bo2, rstd, q_parts, k_parts)
        phase2(nc, sem, psum, values, heads_out, ident, ident_b, k_stage, k_blank, q_parts, k_parts,
               q_rows, k_rows, const_rows, factors)
        phase3(nc, sem, psum, acc, heads_out, ident, wp, out)


def phase1(nc, ph, sem, psum, acc, values, brow, bcol, ident, xc, wq, wk, wx, wi, wb, wo, iota,
           bqs, bo2, rstd, q_parts, k_parts):
    def tmp(name, shape, dt=F32):
        return ph.enter_context(nc.sbuf_tensor(name, shape, dt))

    xn = tmp("xn", [P, 2, CT, C])
    xnT = tmp("xnT", [P, 2, CHUNK])
    proj = tmp("proj", [P, 2, CHUNK])
    res = tmp("res", [P, 2, 2, CHUNK])
    parts = tmp("parts", [P, 2, 3, CHUNK], BF16)
    xa = tmp("xa", [P, 2, CT, C])
    logit = tmp("logit", [P, 2, CT, E])
    top = tmp("top", [P, 2, CT])
    below = tmp("below", [P, CT, E])
    cand = tmp("cand", [P, CT, E])
    first = tmp("first", [P, 2, CT])
    hot = tmp("hot", [P, 2, CT, E])
    swap = tmp("swap", [P, CT, E])
    rest = tmp("rest", [P, CT, E])
    shifted = tmp("shifted", [P, CT, E])
    expd = tmp("expd", [P, CT, E])
    esum = tmp("esum", [P, CT])
    einv = tmp("einv", [P, CT])
    etop = tmp("etop", [P, CT])
    vsum = tmp("vsum", [P, 2, CT])
    gap = tmp("gap", [P, CT])
    egap = tmp("egap", [P, CT])
    masked = tmp("masked", [P, 2, CT, C])
    maskedT = tmp("maskedT", [P, 2, CHUNK])
    relu = tmp("relu", [P, 2, 2, CHUNK])
    hid = tmp("hid", [P, F // P, CHUNK])
    outb = tmp("outb", [P, CT, C])

    xn_ready = sem("xn_ready")
    res_ready = sem("residual_ready")
    xt_ready = sem("xt_in_psum")
    xt_copied = sem("xt_copied")
    qk_ready = sem("qk_in_psum")
    qk_copied = sem("qk_copied")
    vx_ready = sem("vx_in_psum")
    vx_copied = sem("vx_copied")
    split = sem("split_chain")
    parts_out = [sem("q_parts_stored"), sem("k_parts_stored")]
    pick = sem("pick_chain")
    exps = sem("gate_exps")
    mask_ready = sem("masked_ready")
    mt_ready = sem("masked_t_in_psum")
    mt_copied = sem("masked_t_copied")
    in_ready = sem("inter_in_psum")
    in1_used = sem("first_relu")
    in2_used = sem("second_relu")
    hid_ready = sem("hidden_ready")
    y_ready = sem("ffn_in_psum")
    y_chain = sem("ffn_out_chain")
    NF = F // P
    SWAPPED, SHIFTED = 12, 14
    PICK = 18

    with nc.Block() as block:
        @block.gpsimd
        def _(pool):
            def norm(c, par):
                wait(pool, xt_ready, c - 1)
                nc.gpsimd.tensor_tensor(
                    xn[:, par], xc[:, bass.ds(c * CT, CT), :],
                    rstd[:, bass.ds(c * CT, CT)].unsqueeze(2).to_broadcast([P, CT, C]), ALU.mult).then_inc(xn_ready, 1)
                nc.gpsimd.tensor_tensor(
                    acc[:, bass.ds(c * CT, CT), :], acc[:, bass.ds(c * CT, CT), :],
                    brow[:, BP:BP + C].unsqueeze(1).to_broadcast([P, CT, C]), ALU.add).then_inc(res_ready, 1)

            def back(c, par):
                wait(pool, vx_copied, (c + 1) * CT)
                wait(pool, pick, c * PICK + SWAPPED)
                wait(pool, mt_ready, 2 * c)
                for j, sel in enumerate((hot[:, 0], swap[:, :])):
                    nc.gpsimd.tensor_tensor(
                        masked[:, j].rearrange("p n (e r) -> p (n e) r", r=R),
                        xa[:, par].rearrange("p n (e r) -> p (n e) r", r=R),
                        sel.rearrange("p n e -> p (n e)").unsqueeze(2).to_broadcast([P, CT * E, R]),
                        ALU.mult).then_inc(mask_ready, 1)
                for f in range(NF):
                    wait(pool, in2_used, c * NF + f + 1)
                    if f == 0:
                        wait(pool, y_ready, c)
                    nc.gpsimd.tensor_tensor(hid[:, f], relu[:, f % 2, 0], relu[:, f % 2, 1],
                                            ALU.add).then_inc(hid_ready, 1)

            norm(0, 0)

            def body(c, par):
                if not (isinstance(c, int) and c == CHUNKS - 1):
                    norm(c + 1, 1 - par)
                back(c, par)
            chunks(body, pool)

        @block.tensor
        def _(pe):
            def front(c, par):
                pe.wait_ge(xn_ready, c + 1)
                wait(pe, xt_copied, c)
                for n in range(CT):
                    last = nc.tensor.transpose(psum[:, 0, n * P:(n + 1) * P], xn[:, par, n], ident[:, :])
                last.then_inc(xt_ready, 1)
                pe.wait_ge(xt_copied, c + 1)
                for j, w in enumerate((wq, wk)):
                    wait(pe, qk_copied, 2 * c + j - 1)
                    nc.tensor.matmul(psum[:, 1 + j, :], w[:, :], xnT[:, par], start=True, stop=True).then_inc(qk_ready, 1)
                for n in range(CT):
                    wait(pe, vx_copied, c * CT + n - 1)
                    nc.tensor.matmul(psum[:, 3 + n % 2, 0:XW], xnT[:, par, n * P:(n + 1) * P], wx[:, :],
                                     start=True, stop=True).then_inc(vx_ready, 1)

            def back(c, par):
                for j in range(2):
                    pe.wait_ge(mask_ready, 2 * c + j + 1)
                    if j == 0:
                        wait(pe, y_chain, 2 * c - 1)
                    else:
                        pe.wait_ge(mt_copied, 2 * c + 1)
                    for n in range(CT):
                        last = nc.tensor.transpose(psum[:, 5, n * P:(n + 1) * P], masked[:, j, n], ident[:, :])
                    last.then_inc(mt_ready, 1)
                pe.wait_ge(mt_copied, 2 * c + 2)

                def first_expert(f):
                    wait(pe, in2_used, c * NF + f - 1)
                    fs = slice(f * P, (f + 1) * P)
                    nc.tensor.matmul(psum[:, 6 + f % 2, :], wi[:, fs], xnT[:, par], start=True, stop=False)
                    nc.tensor.matmul(psum[:, 6 + f % 2, :], wb[:, fs], maskedT[:, 0], start=False,
                                     stop=True).then_inc(in_ready, 1)

                def second_expert(f):
                    pe.wait_ge(in1_used, c * NF + f + 1)
                    fs = slice(f * P, (f + 1) * P)
                    nc.tensor.matmul(psum[:, 6 + f % 2, :], wb[:, fs], maskedT[:, 1], start=False, stop=True,
                                     skip_group_check=True).then_inc(in_ready, 1)

                for f in range(0, NF, 2):
                    first_expert(f)
                    first_expert(f + 1)
                    second_expert(f)
                    second_expert(f + 1)
                pe.wait_ge(hid_ready, (c + 1) * NF)
                for n in range(CT):
                    for f in range(NF):
                        last = nc.tensor.matmul(psum[:, 5, n * P:(n + 1) * P], hid[:, f, n * P:(n + 1) * P],
                                                wo[:, f], start=(f == 0), stop=(f == NF - 1))
                last.then_inc(y_ready, 1)

            front(0, 0)

            def body(c, par):
                if not (isinstance(c, int) and c == CHUNKS - 1):
                    front(c + 1, 1 - par)
                back(c, par)
            chunks(body, pe)

        @block.scalar
        def _(act):
            def front(c, par):
                act.wait_ge(xt_ready, c + 1)
                wait(act, y_ready, c - 1)
                nc.scalar.activation(xnT[:, par], psum[:, 0, :], ACT.Copy).then_inc(xt_copied, 1)
                for j, (bias, scale) in enumerate(((bqs[:, :], SCALE), (bcol[:, BK:BK + 1], 1.0))):
                    act.wait_ge(qk_ready, 2 * c + j + 1)
                    wait(act, split, 2 * c * 5 - 5 * (1 - j))
                    nc.scalar.activation(proj[:, j], psum[:, 1 + j, :], ACT.Identity, bias=bias,
                                         scale=scale).then_inc(qk_copied, 1)

            def gate(c):
                act.wait_ge(pick, c * PICK + SHIFTED)
                nc.scalar.activation(expd[:, :, :], shifted[:, :, :], ACT.Exp).then_inc(exps, 1)
                nc.scalar.activation(egap[:, :], gap[:, :], ACT.Exp).then_inc(exps, 1)

            def back(c, par):
                for j in range(2):
                    act.wait_ge(mt_ready, 2 * c + j + 1)
                    nc.scalar.activation(maskedT[:, j], psum[:, 5, :], ACT.Copy).then_inc(mt_copied, 1)
                if not (isinstance(c, int) and c == CHUNKS - 1):
                    gate(c + 1)
                for f in range(0, NF, 2):
                    for k in range(2):
                        act.wait_ge(in_ready, 2 * (c * NF + f) + k + 1)
                        wait(act, hid_ready, c * NF + f + k - 1)
                        nc.scalar.activation(relu[:, k, 0], psum[:, 6 + k, :], ACT.Relu,
                                             bias=bcol[:, BI + f + k:BI + f + k + 1]).then_inc(in1_used, 1)
                    for k in range(2):
                        act.wait_ge(in_ready, 2 * (c * NF + f) + k + 3)
                        nc.scalar.activation(relu[:, k, 1], psum[:, 6 + k, :], ACT.Relu,
                                             bias=bcol[:, BI + f + k:BI + f + k + 1]).then_inc(in2_used, 1)

            front(0, 0)
            gate(0)

            def body(c, par):
                if not (isinstance(c, int) and c == CHUNKS - 1):
                    front(c + 1, 1 - par)
                back(c, par)
            chunks(body, act)

        @block.vector
        def _(dve):
            def front(c, par):
                for n in range(CT):
                    dve.wait_ge(vx_ready, c * CT + n + 1)
                    bank = psum[:, 3 + n % 2]
                    nc.vector.tensor_tensor(
                        values[:, bass.ds((c // 2) * PAIRS, PAIRS), bass.ds((c % 2) * CT + n, 1)].rearrange(
                            "p u o a d -> p (u o) (a d)"),
                        bank[:, XV:XV + C].rearrange("p (u w) -> p u w", u=PAIRS),
                        brow[:, BV:BV + C].rearrange("p (u w) -> p u w", u=PAIRS), ALU.add)
                    nc.vector.tensor_tensor(logit[:, par, n], bank[:, XG:XG + E], brow[:, GB:GB + E], ALU.add)
                    if n == 0:
                        wait(dve, mask_ready, 2 * c - 2)
                    nc.vector.tensor_copy(xa[:, par, n], bank[:, XA:XA + C]).then_inc(vx_copied, 1)
                for j in range(2):
                    dve.wait_ge(qk_copied, 2 * c + j + 1)
                    k0 = 2 * 5 * c + 5 * j
                    wait(dve, parts_out[j], 16 * NC * c)
                    nc.vector.tensor_copy(parts[:, j, 0], proj[:, j]).then_inc(split, 1)
                    dve.wait_ge(split, k0 + 1)
                    nc.vector.tensor_tensor(res[:, j, 0], proj[:, j], parts[:, j, 0], ALU.subtract).then_inc(split, 1)
                    dve.wait_ge(split, k0 + 2)
                    nc.vector.tensor_copy(parts[:, j, 1], res[:, j, 0]).then_inc(split, 1)
                    dve.wait_ge(split, k0 + 3)
                    nc.vector.tensor_tensor(res[:, j, 1], res[:, j, 0], parts[:, j, 1], ALU.subtract).then_inc(split, 1)
                    dve.wait_ge(split, k0 + 4)
                    nc.vector.tensor_copy(parts[:, j, 2], res[:, j, 1]).then_inc(split, 1)

            def choose(c, par):
                step = [0]

                def link(ins):
                    ins.then_inc(pick, 1)
                    step[0] += 1
                    dve.wait_ge(pick, c * PICK + step[0])

                def wide(a):
                    return a.unsqueeze(2).to_broadcast([P, CT, E])

                wait(dve, mask_ready, 2 * c)
                dve.wait_ge(vx_copied, CT * (c + 1))
                link(nc.vector.tensor_reduce(top[:, 0], logit[:, par], AX_X, ALU.max))
                source = logit[:, par]
                for j in range(2):
                    link(nc.vector.tensor_tensor(below[:, :, :], source, wide(top[:, j]), ALU.is_lt))
                    link(nc.vector.scalar_tensor_tensor(
                        cand[:, :, :].rearrange("p n e -> p (n e)"), below[:, :, :].rearrange("p n e -> p (n e)"),
                        float(E), iota[:, :, :].rearrange("p n e -> p (n e)"), ALU.mult, ALU.add))
                    link(nc.vector.tensor_reduce(first[:, j], cand[:, :, :], AX_X, ALU.min))
                    link(nc.vector.tensor_tensor(hot[:, j], iota[:, :, :], wide(first[:, j]), ALU.is_equal))
                    if j == 0:
                        link(nc.vector.scalar_tensor_tensor(
                            rest[:, :, :].rearrange("p n e -> p (n e)"), hot[:, 0].rearrange("p n e -> p (n e)"),
                            -3e38, logit[:, par].rearrange("p n e -> p (n e)"), ALU.mult, ALU.add))
                        link(nc.vector.tensor_reduce(top[:, 1], rest[:, :, :], AX_X, ALU.max))
                        source = rest[:, :, :]
                link(nc.vector.tensor_tensor(swap[:, :, :], hot[:, 1], hot[:, 0], ALU.subtract))
                assert step[0] == SWAPPED
                link(nc.vector.tensor_tensor(shifted[:, :, :], logit[:, par], wide(top[:, 0]), ALU.subtract))
                link(nc.vector.tensor_tensor(gap[:, :], top[:, 1], top[:, 0], ALU.subtract))
                assert step[0] == SHIFTED
                dve.wait_ge(exps, 2 * c + 2)
                link(nc.vector.tensor_reduce(esum[:, :], expd[:, :, :], AX_X, ALU.add))
                link(nc.vector.reciprocal(einv[:, :], esum[:, :]))
                link(nc.vector.tensor_scalar(etop[:, :], egap[:, :], 1.0, None, ALU.add))
                link(nc.vector.tensor_tensor(vsum[:, par], etop[:, :], einv[:, :], ALU.mult))
                assert step[0] == PICK

            def back(c, par):
                wait(dve, y_chain, 2 * c)
                dve.wait_ge(y_ready, c + 1)
                nc.vector.tensor_tensor(outb[:, :, :], psum[:, 5, :].rearrange("p (n d) -> p n d", n=CT),
                                        bo2[:, :].unsqueeze(1).to_broadcast([P, CT, C]), ALU.add).then_inc(y_chain, 1)
                dve.wait_ge(y_chain, 2 * c + 1)
                dve.wait_ge(res_ready, c + 1)
                for n in range(CT):
                    tile = acc[:, bass.ds(c * CT + n, 1), :].rearrange("p o d -> p (o d)")
                    last = nc.vector.scalar_tensor_tensor(tile, outb[:, n], vsum[:, par, n:n + 1], tile,
                                                          ALU.mult, ALU.add)
                last.then_inc(y_chain, 1)

            front(0, 0)
            choose(0, 0)

            def body(c, par):
                if not (isinstance(c, int) and c == CHUNKS - 1):
                    front(c + 1, 1 - par)
                    choose(c + 1, 1 - par)
                back(c, par)
            chunks(body, dve)
            dve.wait_ge(y_chain, 2 * CHUNKS)

        @block.sync
        def _(sp):
            def store(c, par):
                for j, (dst, combos) in enumerate(((q_parts, COMBOS_Q), (k_parts, COMBOS_K))):
                    view = dst.rearrange("(b u) a c d t -> b c (u a) d t", b=B)
                    sp.wait_ge(split, 10 * c + 5 * j + 5)
                    for m, part in enumerate(combos):
                        sp.dma_start(
                            view[bass.ds(c // 2, 1), m, :, :, bass.ds((c % 2) * CHUNK, CHUNK)].rearrange(
                                "o g d t -> (o g) d t"),
                            parts[:, j, part]).then_inc(parts_out[j], 16)
            with sp.Fori(0, CHUNKS) as c:
                store(c, 0)
            for j in range(2):
                sp.wait_ge(parts_out[j], 16 * NC * CHUNKS)


def phase2(nc, sem, psum, values, heads_out, ident, ident_b, k_stage, k_blank, q_parts, k_parts,
           q_rows, k_rows, const_rows, factors):
    with ExitStack() as ph:
        def tmp(name, shape, dt=F32):
            return ph.enter_context(nc.sbuf_tensor(name, shape, dt))

        q_stage = tmp("q_stage", [P, RING, T], BF16)
        v_stage = tmp("v_stage", [P, RING, NT, 2, VP])
        probs = tmp("probs", [P, 4, 2, CHUNK])
        factor = tmp("factor", [P, RING, 2, P])
        negmax = tmp("negmax", [P, RING, 2, NT, 2])
        m_min = tmp("m_min", [P, 2, NT])
        m_rest = tmp("m_rest", [P, 2, 2, NT])
        m_pad = tmp("m_pad", [P, P], BF16)
        m_parts = m_pad[:, 0:6 * NT].rearrange("p (a k n) -> p a k n", a=2, k=3)
        nought = tmp("nought", [P, 2, NT])
        m_rows = tmp("m_rows", [2 * 3 * NT, P], BF16)
        y_cols = tmp("y_cols", [P, CHUNK])
        y_inv = tmp("y_inv", [P, CT, 4])

        fixed = sem("fixed_rows_staged")
        staged = [sem(f"unit_staged{r}") for r in range(RING)]
        v_zero = sem("v_stage_blank")
        v_staged = sem("v_staged")
        half_ready = sem("max_scores_in_psum")
        half_used = sem("half_maxima")
        m_ready = sem("maxima_ready")
        m_chain = sem("maxima_parts_chain")
        mt_ready = sem("maxima_t_in_psum")
        mt_copied = sem("maxima_t_copied")
        m_staged = [sem(f"maxima_staged{r}") for r in range(RING)]
        s_ready = sem("scores_in_psum")
        e_ready = sem("exponentials")
        d_ready = sem("diagonal_done")
        pv_done = sem("weighted_values")
        y_copied = sem("y_copied")
        yt_ready = sem("y_t_in_psum")
        y_inverse = sem("y_inverse")
        y_done = sem("y_normalised")

        LOADS = 13
        TILE_STEPS = 2 * NT
        HALVES = 2 * NT * 2
        M_STEPS = 5
        Y_BANK, T_BANK = 6, 7
        y_ps = psum[:, Y_BANK]
        misc = psum[:, T_BANK]

        def number(t, v):
            return t * RING + v

        def slot_of(v):
            return v % RING

        def fill(t, v):
            return t + (v // RING + 1)

        def beyond(t, v):
            return isinstance(t, int) and v >= UNITS

        def units(body, eng):
            body(0, 0)
            body(0, 1)
            with eng.Fori(0, (UNITS - 5) // RING) as t:
                for v in range(2, RING + 2):
                    body(t, v)
            for v in range(UNITS - 3, UNITS):
                body(0, v)

        with nc.Block() as block:
            @block.sync
            def _(sp):
                bits = const_rows.bitcast(BF16)
                q_bias, k_bias = q_rows.bitcast(BF16), k_rows.bitcast(BF16)

                def main(a):
                    return slice(a * MAIN, a * MAIN + QK)

                def most(a):
                    return slice(a * MAIN + QK, (a + 1) * MAIN)

                def bias(a):
                    return slice(2 * MAIN + a * BR, 2 * MAIN + (a + 1) * BR)

                sp.wait_ge(k_blank, 1)
                for slot in range(RING):
                    for a in range(2):
                        sp.dma_start(q_stage[bias(a), slot], q_bias).then_inc(fixed, 16)
                        for form in range(2):
                            sp.dma_start(k_stage[most(a), slot, a, form], bits[0]).then_inc(fixed, 16)

                def stage(t, v):
                    u, slot = number(t, v), slot_of(v)
                    wait(sp, pv_done, (u - RING + 1) * NT)
                    sp.dma_start(factor[:, slot],
                                 factors[bass.ds(u % PAIRS, 1)].rearrange("o p a t -> (o p) a t")).then_inc(staged[slot], 16)
                    for a in range(2):
                        def flat(parts):
                            return parts[bass.ds(u, 1), a].rearrange("o c d t -> (o c d) t")

                        sp.dma_start(q_stage[main(a), slot], flat(q_parts)).then_inc(staged[slot], 16)
                        sp.dma_start(q_stage[most(a), slot], bits[1]).then_inc(staged[slot], 16)
                        for form in range(2):
                            sp.dma_start(k_stage[main(a), slot, a, form], flat(k_parts)).then_inc(staged[slot], 16)
                            sp.dma_start(
                                k_stage[bias(a), slot, a, form],
                                k_bias[bass.ds(u % PAIRS, 1), a, form].rearrange("o r t -> (o r) t")
                            ).then_inc(staged[slot], 16)

                def stage_maxima(t, v):
                    u, slot = number(t, v), slot_of(v)
                    wait(sp, mt_copied, u + 1)
                    for a in range(2):
                        for p in range(MX):
                            row = a * MAIN + QK + p
                            sp.dma_start(
                                q_stage[row:row + 1, slot, :],
                                m_rows[(a * MX + p) * NT:(a * MX + p + 1) * NT, :]).then_inc(m_staged[slot], 16)

                stage(0, 0)
                stage(0, 1)
                stage_maxima(0, 0)

                def body(t, v):
                    if not beyond(t, v + 2):
                        stage(t, v + 2)
                    if not beyond(t, v + 1):
                        stage_maxima(t, v + 1)
                units(body, sp)

            @block.gpsimd
            def _(pool):
                nc.gpsimd.memset(v_stage[:, :, :, :, :], 0.0).then_inc(v_zero, 1)
                pool.wait_ge(v_zero, 1)
                nc.gpsimd.memset(v_stage[:, :, :, :, D:D + 1], 1.0).then_inc(v_zero, 1)
                nc.gpsimd.memset(m_pad[:, :], 0.0).then_inc(v_zero, 1)
                nc.gpsimd.memset(nought[:, :, :], 0.0).then_inc(v_zero, 1)
                pool.wait_ge(v_zero, 4)

                def stage_values(t, v):
                    u, slot = number(t, v), slot_of(v)
                    wait(pool, pv_done, (u - RING + 1) * NT)
                    nc.gpsimd.tensor_copy(
                        v_stage[:, slot, :, :, 0:D].rearrange("p n a d -> p (n a) d"),
                        values[:, bass.ds(u, 1)].rearrange("p o n a d -> p (o n a) d")).then_inc(v_staged, 1)

                def maxima(t, v):
                    u, slot = number(t, v), slot_of(v)
                    k = [0]

                    def link(ins):
                        ins.then_inc(m_chain, 1)
                        k[0] += 1
                        wait(pool, m_chain, u * M_STEPS + k[0])

                    wait(pool, m_ready, u + 1)
                    wait(pool, mt_ready, u)
                    link(nc.gpsimd.tensor_tensor(m_parts[:, :, 0], m_min[:, :, :], nought[:, :, :], ALU.add))
                    link(nc.gpsimd.tensor_tensor(m_rest[:, 0], m_min[:, :, :], m_parts[:, :, 0], ALU.subtract))
                    link(nc.gpsimd.tensor_tensor(m_parts[:, :, 1], m_rest[:, 0], nought[:, :, :], ALU.add))
                    link(nc.gpsimd.tensor_tensor(m_rest[:, 1], m_rest[:, 0], m_parts[:, :, 1], ALU.subtract))
                    link(nc.gpsimd.tensor_tensor(m_parts[:, :, 2], m_rest[:, 1], nought[:, :, :], ALU.add))

                stage_values(0, 0)
                stage_values(0, 1)
                maxima(0, 0)

                def body(t, v):
                    u, slot = number(t, v), slot_of(v)
                    for i in range(NT):
                        c = i // CT
                        wait(pool, e_ready, u * TILE_STEPS + 2 * i + c + 1)
                        tile = probs[:, (2 * i + c) % 4, :, (i % CT) * P:(i % CT + 1) * P]
                        nc.gpsimd.tensor_tensor(
                            tile, tile,
                            factor[:, slot],
                            ALU.mult).then_inc(d_ready, 1)
                        if i == 1 and not beyond(t, v + 2):
                            stage_values(t, v + 2)
                        if i == NT // 2 and not beyond(t, v + 1):
                            maxima(t, v + 1)
                units(body, pool)

            @block.tensor
            def _(pe):
                def max_tile(t, v, a, j):
                    u, slot = number(t, v), slot_of(v)
                    """Scores of head a's query tile j, both halves of the keys."""
                    if j == 0 and a == 0:
                        pe.wait_ge(staged[slot], fill(t, v) * (LOADS * 16))
                    for h in range(2):
                        m = u * HALVES + (a * NT + j) * 2 + h
                        wait(pe, half_used, m - 1)
                        for s0, s1, form, rows in regions_by_keys(j, h):
                            ins = nc.tensor.matmul(
                                psum[:, 4 + h, s0 - h * 512:s1 - h * 512],
                                q_stage[0:rows, slot, j * P:(j + 1) * P],
                                k_stage[0:rows, slot, a, form, s0:s1], start=True, stop=True)
                        ins.then_inc(half_ready, 1)

                def scores(t, v, i, c):
                    u, slot = number(t, v), slot_of(v)
                    n = 2 * i + c
                    if n == 0:
                        pe.wait_ge(m_staged[slot], fill(t, v) * (6 * 16))
                    wait(pe, e_ready, u * TILE_STEPS + n - 1)
                    for t0, t1, form, rows in regions_by_queries(i, c):
                        for a in range(2):
                            ins = nc.tensor.matmul(
                                psum[:, 2 * c + a, t0 - c * 512:t1 - c * 512],
                                k_stage[0:rows, slot, a, form, i * P:(i + 1) * P],
                                q_stage[0:rows, slot, t0:t1], start=True, stop=True)
                    ins.then_inc(s_ready, 1)

                def weigh(t, v, i):
                    u, slot = number(t, v), slot_of(v)
                    if i == 0:
                        pe.wait_ge(v_staged, u + 1)
                        wait(pe, y_copied, u)
                    pe.wait_ge(e_ready, u * TILE_STEPS + 2 * i + 2)
                    pe.wait_ge(d_ready, u * NT + i + 1)
                    for a in range(2):
                        for c in range(2):
                            g = 32 * (2 * a + c)
                            ins = nc.tensor.matmul(y_ps[g:g + VP, :], v_stage[:, slot, i, a, :],
                                                   probs[:, (2 * i + c) % 4, a, :],
                                                   start=(i == 0), stop=(i == NT - 1))
                    ins.then_inc(pv_done, 1)

                def turn_y(t, v):
                    u = number(t, v)
                    pe.wait_ge(y_copied, u + 1)
                    wait(pe, y_done, 2 * u)
                    pe.wait_ge(mt_copied, UNITS if beyond(t, v + 1) else u + 2)
                    for q in range(CT):
                        ins = nc.tensor.transpose(misc[:, q * P:(q + 1) * P], y_cols[:, q * P:(q + 1) * P], ident[:, :])
                    ins.then_inc(yt_ready, 1)

                def turn_maxima(t, v):
                    u = number(t, v)
                    wait(pe, y_done, 2 * (u - 1))
                    pe.wait_ge(m_chain, (u + 1) * M_STEPS)
                    nc.tensor.transpose(misc.bitcast(BF16)[:, 0:P], m_pad[:, :],
                                        ident_b[:, :]).then_inc(mt_ready, 1)

                pe.wait_ge(fixed, 16 * RING * 6)
                for j in range(NT):
                    max_tile(0, 0, 0, j)
                for j in range(NT):
                    max_tile(0, 0, 1, j)
                for j in range(NT):
                    max_tile(0, 1, 0, j)
                turn_maxima(0, 0)

                def body(t, v):
                    start = isinstance(t, int) and v == 0
                    for i in range(NT):
                        for c in range(2):
                            scores(t, v, i, c)
                        for j in range(2 * (i % CT), 2 * (i % CT) + 2):
                            if i < CT and not beyond(t, v + 1):
                                max_tile(t, v + 1, 1, j)
                            if i >= CT and not beyond(t, v + 2):
                                max_tile(t, v + 2, 0, j)
                        if i > 0:
                            weigh(t, v, i - 1)
                        elif not start:
                            weigh(t, v - 1, NT - 1)
                        if i == 2 and not start:
                            turn_y(t, v - 1)
                        if i == 6 and not beyond(t, v + 1):
                            turn_maxima(t, v + 1)
                units(body, pe)
                weigh(0, UNITS - 1, NT - 1)
                turn_y(0, UNITS - 1)

            @block.scalar
            def _(act):
                def copy_y(t, v):
                    u = number(t, v)
                    act.wait_ge(pv_done, (u + 1) * NT)
                    wait(act, yt_ready, u)
                    nc.scalar.activation(y_cols[:, :], y_ps, ACT.Copy).then_inc(y_copied, 1)

                def copy_maxima(t, v):
                    u = number(t, v)
                    act.wait_ge(mt_ready, u + 1)
                    if not (isinstance(t, int) and v == 0):
                        act.wait_ge(m_staged[slot_of(v - 1)], fill(t, v - 1) * (6 * 16))
                    nc.scalar.activation(m_rows[:, :], misc.bitcast(BF16)[0:48, 0:P], ACT.Copy).then_inc(mt_copied, 1)

                copy_maxima(0, 0)

                def body(t, v):
                    u = number(t, v)
                    for i in range(NT):
                        for c in range(2):
                            n = 2 * i + c
                            act.wait_ge(s_ready, u * TILE_STEPS + n + 1)
                            wait(act, pv_done, u * NT + i - 1)
                            nc.scalar.activation(
                                probs[:, n % 4], psum[:, 2 * c:2 * c + 2, :], ACT.Exp).then_inc(e_ready, 1)
                        if i == 1 and not (isinstance(t, int) and v == 0):
                            copy_y(t, v - 1)
                        if i == 6 and not beyond(t, v + 1):
                            copy_maxima(t, v + 1)
                units(body, act)
                copy_y(0, UNITS - 1)

            @block.vector
            def _(dve):
                def reduce(t, v, a, j):
                    u, slot = number(t, v), slot_of(v)
                    for h in range(2):
                        dve.wait_ge(half_ready, u * HALVES + (a * NT + j) * 2 + h + 1)
                        nc.vector.tensor_reduce(negmax[:, slot, a, j, h:h + 1], psum[:, 4 + h, :], AX_X, ALU.max,
                                                negate=True).then_inc(half_used, 1)
                    if a == 1 and j == NT - 1:
                        dve.wait_ge(half_used, (u + 1) * HALVES)
                        wait(dve, m_chain, u * M_STEPS)
                        nc.vector.tensor_tensor(m_min[:, :, :], negmax[:, slot, :, :, 0], negmax[:, slot, :, :, 1],
                                                ALU.min).then_inc(m_ready, 1)

                def norm_y(t, v):
                    u = number(t, v)
                    wait(dve, y_done, 2 * u)
                    dve.wait_ge(yt_ready, u + 1)
                    grid = misc.rearrange("p (q g w) -> p q g w", q=CT, g=4)
                    nc.vector.reciprocal(y_inv[:, :, :], grid[:, :, :, D]).then_inc(y_inverse, 1)
                    dve.wait_ge(y_inverse, u + 1)
                    for a in range(2):
                        for c in range(2):
                            dst = heads_out[:, bass.ds(u, 1), c * CT:(c + 1) * CT, a * D:(a + 1) * D]
                            ins = nc.vector.tensor_tensor(
                                dst.rearrange("p o n d -> p (o n) d"), grid[:, :, 2 * a + c, 0:D],
                                y_inv[:, :, 2 * a + c].unsqueeze(2).to_broadcast([P, CT, D]), ALU.mult)
                        ins.then_inc(y_done, 1)

                for j in range(NT):
                    reduce(0, 0, 0, j)
                for j in range(NT):
                    reduce(0, 0, 1, j)
                for j in range(NT):
                    reduce(0, 1, 0, j)

                def body(t, v):
                    for i in range(NT):
                        for j in range(2 * (i % CT), 2 * (i % CT) + 2):
                            if i < CT and not beyond(t, v + 1):
                                reduce(t, v + 1, 1, j)
                            if i >= CT and not beyond(t, v + 2):
                                reduce(t, v + 2, 0, j)
                        if i == 2 and not (isinstance(t, int) and v == 0):
                            norm_y(t, v - 1)
                units(body, dve)
                norm_y(0, UNITS - 1)
                dve.wait_ge(y_done, 2 * UNITS)


def regions_by_keys(j, h):
    lo, hi = h * 512, h * 512 + 512
    spans = ((0, j * P, 1, ALL), (j * P, (j + 1) * P, 0, ALL), ((j + 1) * P, T, 0, 2 * MAIN))
    return [(max(lo, s0), min(hi, s1), form, rows) for s0, s1, form, rows in spans if max(lo, s0) < min(hi, s1)]


def regions_by_queries(i, c):
    lo, hi = c * 512, c * 512 + 512
    spans = ((0, i * P, 0, 2 * MAIN), (i * P, (i + 1) * P, 0, ALL), ((i + 1) * P, T, 1, ALL))
    return [(max(lo, t0), min(hi, t1), form, rows) for t0, t1, form, rows in spans if max(lo, t0) < min(hi, t1)]


def phase3(nc, sem, psum, acc, heads_out, ident, wp, out):
    with ExitStack() as ph:
        gathered = ph.enter_context(nc.sbuf_tensor("gathered", [P, 2, CT, C], F32))
        turned = ph.enter_context(nc.sbuf_tensor("turned", [P, 2, CHUNK], F32))
        g_ready = sem("gathered_ready")
        t_ready = sem("turned_in_psum")
        t_copied = sem("turned_copied")
        p_ready = sem("projected")
        p_added = sem("projection_added")
        stored = sem("stored")
        out_v = out.rearrange("b (n p) d -> p (b n) d", p=P)

        with nc.Block() as block:
            @block.gpsimd
            def _(pool):
                def body(c, par):
                    wait(pool, t_ready, c - 1)
                    nc.gpsimd.tensor_copy(
                        gathered[:, par].rearrange("p n (u w) -> p n u w", u=PAIRS),
                        heads_out[:, bass.ds((c // 2) * PAIRS, PAIRS), par * CT:(par + 1) * CT].rearrange(
                            "p u n w -> p n u w")).then_inc(g_ready, 1)
                chunks(body, pool, 2)

            @block.tensor
            def _(pe):
                def turn(c, par):
                    pe.wait_ge(g_ready, c + 1)
                    wait(pe, t_copied, c - 1)
                    for n in range(CT):
                        ins = nc.tensor.transpose(psum[:, par, n * P:(n + 1) * P], gathered[:, par, n], ident[:, :])
                    ins.then_inc(t_ready, 1)

                turn(0, 0)

                def body(c, par):
                    if not (isinstance(c, int) and c == CHUNKS - 1):
                        turn(c + 1, 1 - par)
                    pe.wait_ge(t_copied, c + 1)
                    wait(pe, p_added, c - 1)
                    for n in range(CT):
                        ins = nc.tensor.matmul(psum[:, 2 + par, n * P:(n + 1) * P], turned[:, par, n * P:(n + 1) * P],
                                               wp[:, :], start=True, stop=True)
                    ins.then_inc(p_ready, 1)
                chunks(body, pe, 2)

            @block.scalar
            def _(act):
                def body(c, par):
                    act.wait_ge(t_ready, c + 1)
                    wait(act, p_ready, c - 1)
                    nc.scalar.activation(turned[:, par], psum[:, par], ACT.Copy).then_inc(t_copied, 1)
                chunks(body, act, 2)

            @block.vector
            def _(dve):
                def body(c, par):
                    dve.wait_ge(p_ready, c + 1)
                    tiles = acc[:, bass.ds(c * CT, CT), :].rearrange("p n d -> p (n d)")
                    nc.vector.tensor_tensor(tiles, psum[:, 2 + par], tiles, ALU.add).then_inc(p_added, 1)
                chunks(body, dve, 2)

            @block.sync
            def _(sp):
                def body(c, par):
                    sp.wait_ge(p_added, c + 1)
                    sp.dma_start(out_v[:, bass.ds(c * CT, CT), :], acc[:, bass.ds(c * CT, CT), :]).then_inc(stored, 16)
                chunks(body, sp, 2)
                sp.wait_ge(stored, 16 * CHUNKS)


def rounded(v):
    bits = np.asarray(v, np.float32).view(np.uint32)
    return ((bits + 0x7FFF + ((bits >> 16) & 1)) & 0xFFFF0000).astype(np.uint32).view(np.float32)


def constants():
    def parts3(v):
        v = np.asarray(v, np.float32)
        a = rounded(v)
        b = rounded(v - a)
        return a, b, rounded(v - a - b)

    def bits(v):
        return (rounded(v).view(np.uint32) >> 16).astype(np.uint16)

    start = 2.0 ** (-2.0 ** (-(np.log2(H) - 3)))
    slopes = np.array([start * start ** i for i in range(H)]).astype(np.float32)
    pos = np.arange(T)
    lane = pos % P
    steps = range(1, P // STEP)
    q_rows = np.zeros((BR, T), np.float32)
    for m in steps:
        q_rows[m - 1] = lane >= m * STEP
    q_rows[3:6] = 1.0
    q_rows[6:9] = lane
    q_rows[9:12] = (pos // P - NT // 2) * P
    k_rows = np.zeros((H, 2, BR, T), np.float32)
    factors = np.zeros((P, H, P), np.float32)
    s_l, t_l = np.arange(P)[:, None], np.arange(P)[None, :]
    for h in range(H):
        step = rounded(slopes[h:h + 1] * np.float32(STEP))[0]
        for m in steps:
            k_rows[h, 0, m - 1] = np.where(lane < m * STEP, -step, 0.0)
        k_rows[h, 1, 3:6] = parts3(slopes[h] * (pos - T // 2).astype(np.float32))
        for p, part in enumerate(parts3(slopes[h:h + 1])):
            k_rows[h, 1, 6 + p] = -part[0]
            k_rows[h, 1, 9 + p] = -part[0]
        stairs = sum(((s_l < m * STEP) & (t_l >= m * STEP)).astype(np.float64) for m in steps)
        factors[:, h] = np.exp(float(slopes[h]) * np.minimum(s_l - t_l, 0) + float(step) * stairs)
    const_rows = np.stack([np.ones((MX, T), np.float32), np.zeros((MX, T), np.float32)])
    return dict(ident_in=np.eye(P, dtype=np.float32),
                iota_in=np.ascontiguousarray(np.broadcast_to(np.arange(E, dtype=np.float32), (P, CT, E))),
                q_rows=bits(q_rows), k_rows=bits(k_rows).reshape(PAIRS, 2, 2, BR, T),
                const_rows=bits(const_rows),
                factors=factors.reshape(P, PAIRS, 2, P).transpose(1, 0, 2, 3))


def kernel(L0_attn_x, L0_attn_W_qkv, L0_attn_b_qkv, L0_attn_W_proj, L0_attn_b_proj, L0_ffn_wi, L0_ffn_bi,
           L0_ffn_wo, L0_ffn_bo, L0_ffn_lora_A, L0_ffn_lora_B, L0_ffn_gate_w, L0_ffn_gate_b):
    import concourse.bacc as _bacc
    from concourse.bass_utils import run_bass_kernel_spmd as _run

    w_qkv, b_qkv = np.asarray(L0_attn_W_qkv), np.asarray(L0_attn_b_qkv)
    row = np.concatenate([b_qkv[2 * C:], np.asarray(L0_attn_b_proj), np.asarray(L0_ffn_bo),
                          np.asarray(L0_ffn_gate_b)])
    laid = dict(
        x=np.asarray(L0_attn_x),
        w_q=w_qkv[:, 0:C], w_k=w_qkv[:, C:2 * C],
        w_x=np.concatenate([w_qkv[:, 2 * C:], np.asarray(L0_ffn_lora_A).reshape(E * R, C).T,
                            np.asarray(L0_ffn_gate_w).T], axis=1),
        w_i=np.asarray(L0_ffn_wi).T,
        w_b=np.asarray(L0_ffn_lora_B).transpose(0, 2, 1).reshape(E * R, F),
        w_o=np.asarray(L0_ffn_wo).T.reshape(F // P, P, C).transpose(1, 0, 2),
        w_p=np.asarray(L0_attn_W_proj),
        bias_rows=np.broadcast_to(row, (P, row.shape[0])),
        bias_cols=np.concatenate([b_qkv[0:2 * C].reshape(2, C).T, np.asarray(L0_ffn_bi).reshape(F // P, P).T], axis=1),
    )
    laid.update(constants())
    nc = _bacc.Bacc("TRN2", target_bir_lowering=False, num_devices=1)
    arrays, args = {}, {}
    for name, a in laid.items():
        a = np.ascontiguousarray(a)
        arrays[f"in_{name}"] = a
        args[name] = nc.dram_tensor(f"in_{name}", a.shape, mybir.dt.from_np(a.dtype), kind="ExternalInput").ap()
    args["out"] = nc.dram_tensor("out", (B, T, C), F32, kind="ExternalOutput").ap()
    build(nc, **args)
    r = _run(nc, [arrays], core_ids=[0])
    return r.results[0]["out"]
```

```python
from contextlib import ExitStack

import numpy as np

import concourse.bass as bass
from concourse import mybir

F32 = mybir.dt.float32
BF16 = mybir.dt.bfloat16
ALU = mybir.AluOpType
ACT = mybir.ActivationFunctionType
AX_X = mybir.AxisListType.X

P = 128
B, T, C, H, D = 4, 1024, 128, 16, 8
E, R, F = 8, 16, 512
NT = T // P
TILES = B * NT
CT = 4
CHUNK = CT * P
CHUNKS = TILES // CT
PAIRS = H // 2
UNITS = B * PAIRS
COMBOS_Q = (0, 0, 1, 1, 0, 2)
COMBOS_K = (0, 1, 0, 1, 2, 0)
NC = len(COMBOS_Q)
QK = NC * D
MX = 3
BR = 12
MAIN = 2 * (QK + MX)
ALL = MAIN + 2 * BR
STEP = 32
RING = 3
PROBS = 8
LAG = 2
VP = 32
EPS = 1e-5
SCALE = 1.0 / float(np.sqrt(D))
BV, BP, BO, GB = 0, C, 2 * C, 3 * C
BQ, BK, BI = 0, 1, 2
XV, XA, XG = 0, C, 2 * C
XW = 2 * C + E


def wait(eng, sem, value):
    if isinstance(value, int) and value <= 0:
        return
    eng.wait_ge(sem, value)


def chunks(body, eng, ends=1):
    for c in range(ends):
        body(c, c % 2)
    with eng.Fori(0, CHUNKS // 2 - ends) as t:
        for k in range(ends, ends + 2):
            body(t * 2 + k, k % 2)
    for c in range(CHUNKS - ends, CHUNKS):
        body(c, c % 2)


def build(nc, x, w_q, w_k, w_x, w_i, w_b, w_o, w_p, bias_rows, bias_cols, ident_in, iota_in,
          q_rows, k_rows, const_rows, factors, out):
    with ExitStack() as ctx:
        def sb(name, shape, dt=F32):
            return ctx.enter_context(nc.sbuf_tensor(name, shape, dt))

        def sem(name):
            return ctx.enter_context(nc.semaphore(name))

        q_parts = nc.dram_tensor("q_parts", (UNITS, 2, NC, D, T), BF16, kind="Internal").ap()
        k_parts = nc.dram_tensor("k_parts", (UNITS, 2, NC, D, T), BF16, kind="Internal").ap()

        acc = sb("acc", [P, TILES, C])
        values = sb("values", [P, UNITS, NT, 2, D])
        heads_out = sb("heads_out", [P, UNITS, NT, 2 * D])
        brow = sb("brow", [P, 3 * C + E])
        bcol = sb("bcol", [P, 6])
        ident = sb("ident", [P, P])
        ident_b = sb("ident_b", [P, P], BF16)
        wp = sb("wp", [P, C])

        k_stage = sb("k_stage", [P, RING, 2, 2, T], BF16)

        psum = ctx.enter_context(nc.psum_tensor("psum", [P, 8, 512], F32))

        with ExitStack() as ph:
            def tmp(name, shape, dt=F32):
                return ph.enter_context(nc.sbuf_tensor(name, shape, dt))

            xc = tmp("xc", [P, TILES, C])
            wq = tmp("wq", [P, C])
            wk = tmp("wk", [P, C])
            wx = tmp("wx", [P, XW])
            wi = tmp("wi", [P, F])
            wb = tmp("wb", [P, F])
            wo = tmp("wo", [P, F // P, C])
            iota = tmp("iota", [P, CT, E])
            bqs = tmp("bqs", [P, 1])
            rstd = tmp("rstd", [P, TILES])
            bo2 = tmp("bo2", [P, C])
            sums = tmp("sums", [P, TILES])
            mean = tmp("mean", [P, TILES])
            ssq = tmp("ssq", [P, TILES])
            junk = tmp("junk", [P, TILES, C])
            var = tmp("var", [P, TILES])
            root = tmp("root", [P, TILES])
            rinv = tmp("rinv", [P, TILES])
            quo = tmp("quo", [P, TILES])
            root2 = tmp("root2", [P, TILES])

            s_x = [sem(f"x_loaded{b}") for b in range(B)]
            s_w = sem("weights_loaded")
            s_sum = sem("row_sums")
            s_mean = sem("means")
            s_xc = sem("centred")
            s_ssq = sem("squares_summed")
            s_chain = sem("variance_chain")
            s_root = sem("rooted")
            s_const = sem("constants_made")
            k_blank = sem("k_stage_blank")
            W_LOADS = 11
            with nc.Block() as block:
                x_v = x.rearrange("b (n p) d -> b p n d", p=P)

                @block.sync
                def _(sp):
                    for b in range(B):
                        sp.dma_start(acc[:, b * NT:(b + 1) * NT, :], x_v[b]).then_inc(s_x[b], 16)
                    for dst, src in ((wq, w_q), (wk, w_k), (wx, w_x), (wi, w_i), (wb, w_b), (wp, w_p),
                                     (brow, bias_rows), (bcol, bias_cols), (ident, ident_in)):
                        sp.dma_start(dst[:, :], src).then_inc(s_w, 16)
                    sp.dma_start(wo[:, :, :], w_o).then_inc(s_w, 16)
                    sp.dma_start(iota[:, :, :], iota_in).then_inc(s_w, 16)

                @block.gpsimd
                def _(pool):
                    nc.gpsimd.memset(k_stage[:, :, :, :, :], 0.0).then_inc(k_blank, 1)

                @block.vector
                def _(dve):
                    for b in range(B):
                        g = slice(b * NT, (b + 1) * NT)
                        dve.wait_ge(s_x[b], 16)
                        nc.vector.tensor_reduce(sums[:, g], acc[:, g, :], AX_X, ALU.add).then_inc(s_sum, 1)
                        dve.wait_ge(s_sum, b + 1)
                        nc.vector.tensor_scalar(mean[:, g], sums[:, g], 1.0 / C, None, ALU.mult).then_inc(s_mean, 1)
                        dve.wait_ge(s_mean, b + 1)
                        nc.vector.tensor_tensor(
                            xc[:, g, :], acc[:, g, :], mean[:, g].unsqueeze(2).to_broadcast([P, NT, C]),
                            ALU.subtract).then_inc(s_xc, 1)
                    dve.wait_ge(s_ssq, TILES)
                    nc.vector.tensor_scalar(var[:, :], ssq[:, :], 1.0 / C, EPS, ALU.mult, ALU.add).then_inc(s_chain, 1)
                    dve.wait_ge(s_root, 1)
                    nc.vector.reciprocal(rinv[:, :], root[:, :]).then_inc(s_chain, 1)
                    dve.wait_ge(s_chain, 2)
                    nc.vector.tensor_tensor(quo[:, :], var[:, :], rinv[:, :], ALU.mult).then_inc(s_chain, 1)
                    dve.wait_ge(s_chain, 3)
                    nc.vector.tensor_tensor(sums[:, :], quo[:, :], root[:, :], ALU.add).then_inc(s_chain, 1)
                    dve.wait_ge(s_chain, 4)
                    nc.vector.tensor_scalar(root2[:, :], sums[:, :], 0.5, None, ALU.mult).then_inc(s_chain, 1)
                    dve.wait_ge(s_chain, 5)
                    nc.vector.reciprocal(rstd[:, :], root2[:, :]).then_inc(s_chain, 1)
                    dve.wait_ge(s_w, 16 * W_LOADS)
                    nc.vector.tensor_copy(ident_b[:, :], ident[:, :]).then_inc(s_const, 1)
                    nc.vector.tensor_scalar(bqs[:, :], bcol[:, BQ:BQ + 1], SCALE, None, ALU.mult).then_inc(s_const, 1)
                    nc.vector.tensor_scalar(bo2[:, :], brow[:, BO:BO + C], 2.0, None, ALU.mult).then_inc(s_const, 1)

                @block.scalar
                def _(act):
                    for n in range(TILES):
                        act.wait_ge(s_xc, n // NT + 1)
                        nc.scalar.activation(junk[:, n, :], xc[:, n, :], ACT.Square,
                                             accum_out=ssq[:, n:n + 1]).then_inc(s_ssq, 1)
                    act.wait_ge(s_chain, 1)
                    nc.scalar.activation(root[:, :], var[:, :], ACT.Sqrt).then_inc(s_root, 1)

            phase1(nc, ph, sem, psum, acc, values, brow, bcol, ident, xc, wq, wk, wx, wi, wb, wo, iota,
                   bqs, bo2, rstd, q_parts, k_parts)
        phase2(nc, sem, psum, values, heads_out, ident, ident_b, k_stage, k_blank, q_parts, k_parts,
               q_rows, k_rows, const_rows, factors)
        phase3(nc, sem, psum, acc, heads_out, ident, wp, out)


def phase1(nc, ph, sem, psum, acc, values, brow, bcol, ident, xc, wq, wk, wx, wi, wb, wo, iota,
           bqs, bo2, rstd, q_parts, k_parts):
    def tmp(name, shape, dt=F32):
        return ph.enter_context(nc.sbuf_tensor(name, shape, dt))

    xn = tmp("xn", [P, 2, CT, C])
    xnT = tmp("xnT", [P, 2, CHUNK])
    proj = tmp("proj", [P, 2, CHUNK])
    res = tmp("res", [P, 2, 2, CHUNK])
    parts = tmp("parts", [P, 2, 3, CHUNK], BF16)
    xa = tmp("xa", [P, 2, CT, C])
    logit = tmp("logit", [P, 2, CT, E])
    top = tmp("top", [P, 2, CT])
    below = tmp("below", [P, CT, E])
    cand = tmp("cand", [P, CT, E])
    first = tmp("first", [P, 2, CT])
    hot = tmp("hot", [P, 2, CT, E])
    swap = tmp("swap", [P, CT, E])
    rest = tmp("rest", [P, CT, E])
    shifted = tmp("shifted", [P, CT, E])
    expd = tmp("expd", [P, CT, E])
    esum = tmp("esum", [P, CT])
    einv = tmp("einv", [P, CT])
    etop = tmp("etop", [P, CT])
    vsum = tmp("vsum", [P, 2, CT])
    gap = tmp("gap", [P, CT])
    egap = tmp("egap", [P, CT])
    masked = tmp("masked", [P, 2, CT, C])
    maskedT = tmp("maskedT", [P, 2, CHUNK])
    relu = tmp("relu", [P, 2, 2, CHUNK])
    hid = tmp("hid", [P, F // P, CHUNK])
    outb = tmp("outb", [P, CT, C])

    xn_ready = sem("xn_ready")
    res_ready = sem("residual_ready")
    xt_ready = sem("xt_in_psum")
    xt_copied = sem("xt_copied")
    qk_ready = sem("qk_in_psum")
    qk_copied = sem("qk_copied")
    vx_ready = sem("vx_in_psum")
    vx_copied = sem("vx_copied")
    split = sem("split_chain")
    parts_out = [sem("q_parts_stored"), sem("k_parts_stored")]
    pick = sem("pick_chain")
    exps = sem("gate_exps")
    mask_ready = sem("masked_ready")
    mt_ready = sem("masked_t_in_psum")
    mt_copied = sem("masked_t_copied")
    in_ready = sem("inter_in_psum")
    in1_used = sem("first_relu")
    in2_used = sem("second_relu")
    hid_ready = sem("hidden_ready")
    y_ready = sem("ffn_in_psum")
    y_chain = sem("ffn_out_chain")
    NF = F // P
    SWAPPED, SHIFTED = 12, 14
    PICK = 18

    def beyond(c):
        return isinstance(c, int) and c >= CHUNKS

    with nc.Block() as block:
        @block.gpsimd
        def _(pool):
            def norm(c, par):
                wait(pool, xt_ready, c - 1)
                nc.gpsimd.tensor_tensor(
                    xn[:, par], xc[:, bass.ds(c * CT, CT), :],
                    rstd[:, bass.ds(c * CT, CT)].unsqueeze(2).to_broadcast([P, CT, C]), ALU.mult).then_inc(xn_ready, 1)

            def residual(c):
                nc.gpsimd.tensor_tensor(
                    acc[:, bass.ds(c * CT, CT), :], acc[:, bass.ds(c * CT, CT), :],
                    brow[:, BP:BP + C].unsqueeze(1).to_broadcast([P, CT, C]), ALU.add).then_inc(res_ready, 1)

            def mask(c, par):
                wait(pool, vx_copied, (c + 1) * CT)
                wait(pool, pick, c * PICK + SWAPPED)
                wait(pool, mt_ready, 2 * c)
                for j, sel in enumerate((hot[:, 0], swap[:, :])):
                    nc.gpsimd.tensor_tensor(
                        masked[:, j].rearrange("p n (e r) -> p (n e) r", r=R),
                        xa[:, par].rearrange("p n (e r) -> p (n e) r", r=R),
                        sel.rearrange("p n e -> p (n e)").unsqueeze(2).to_broadcast([P, CT * E, R]),
                        ALU.mult).then_inc(mask_ready, 1)

            def hidden(c):
                for f in range(NF):
                    wait(pool, in2_used, c * NF + f + 1)
                    if f == 0:
                        wait(pool, y_ready, c)
                    nc.gpsimd.tensor_tensor(hid[:, f], relu[:, f % 2, 0], relu[:, f % 2, 1],
                                            ALU.add).then_inc(hid_ready, 1)

            norm(0, 0)
            norm(1, 1)
            mask(0, 0)

            def body(c, par):
                if not beyond(c + 2):
                    norm(c + 2, par)
                if not beyond(c + 1):
                    mask(c + 1, 1 - par)
                hidden(c)
                residual(c)
            chunks(body, pool, 2)

        @block.tensor
        def _(pe):
            def turn_x(c, par):
                pe.wait_ge(xn_ready, c + 1)
                wait(pe, xt_copied, c)
                for n in range(CT):
                    last = nc.tensor.transpose(psum[:, 0, n * P:(n + 1) * P], xn[:, par, n], ident[:, :])
                last.then_inc(xt_ready, 1)

            def products(c, par):
                pe.wait_ge(xt_copied, c + 1)
                for j, w in enumerate((wq, wk)):
                    wait(pe, qk_copied, 2 * c + j - 1)
                    nc.tensor.matmul(psum[:, 1 + j, :], w[:, :], xnT[:, par], start=True, stop=True).then_inc(qk_ready, 1)
                if not (isinstance(c, int) and c < 2):
                    pe.wait_ge(mt_copied, 2 * c)
                for n in range(CT):
                    wait(pe, vx_copied, c * CT + n - 1)
                    nc.tensor.matmul(psum[:, 3 + n % 2, 0:XW], xnT[:, par, n * P:(n + 1) * P], wx[:, :],
                                     start=True, stop=True).then_inc(vx_ready, 1)

            def turn_masked(c):
                if isinstance(c, int) and c == 0:
                    pe.wait_ge(vx_copied, 2 * CT)
                for j in range(2):
                    pe.wait_ge(mask_ready, 2 * c + j + 1)
                    for n in range(CT):
                        last = nc.tensor.transpose(psum[:, 3 + j, n * P:(n + 1) * P], masked[:, j, n], ident[:, :])
                    last.then_inc(mt_ready, 1)

            def hidden(c, par):
                pe.wait_ge(mt_copied, 2 * c + 2)

                def first_expert(f):
                    wait(pe, in2_used, c * NF + f - 1)
                    fs = slice(f * P, (f + 1) * P)
                    nc.tensor.matmul(psum[:, 6 + f % 2, :], wi[:, fs], xnT[:, par], start=True, stop=False)
                    nc.tensor.matmul(psum[:, 6 + f % 2, :], wb[:, fs], maskedT[:, 0], start=False,
                                     stop=True).then_inc(in_ready, 1)

                def second_expert(f):
                    pe.wait_ge(in1_used, c * NF + f + 1)
                    fs = slice(f * P, (f + 1) * P)
                    nc.tensor.matmul(psum[:, 6 + f % 2, :], wb[:, fs], maskedT[:, 1], start=False, stop=True,
                                     skip_group_check=True).then_inc(in_ready, 1)

                for f in range(0, NF, 2):
                    first_expert(f)
                    first_expert(f + 1)
                    second_expert(f)
                    second_expert(f + 1)

            def output(c):
                wait(pe, y_chain, 2 * c - 1)
                pe.wait_ge(hid_ready, (c + 1) * NF)
                for n in range(CT):
                    for f in range(NF):
                        last = nc.tensor.matmul(psum[:, 5, n * P:(n + 1) * P], hid[:, f, n * P:(n + 1) * P],
                                                wo[:, f], start=(f == 0), stop=(f == NF - 1))
                last.then_inc(y_ready, 1)

            for c in range(2):
                turn_x(c, c)
                products(c, c)
            turn_masked(0)

            def body(c, par):
                hidden(c, par)
                if not beyond(c + 2):
                    turn_x(c + 2, par)
                if not beyond(c + 1):
                    turn_masked(c + 1)
                if not beyond(c + 2):
                    products(c + 2, par)
                output(c)
            chunks(body, pe, 2)

        @block.scalar
        def _(act):
            def copy_x(c, par):
                act.wait_ge(xt_ready, c + 1)
                wait(act, in_ready, 2 * NF * (c - 1))
                nc.scalar.activation(xnT[:, par], psum[:, 0, :], ACT.Copy).then_inc(xt_copied, 1)

            def copy_qk(c):
                for j, (bias, scale) in enumerate(((bqs[:, :], SCALE), (bcol[:, BK:BK + 1], 1.0))):
                    act.wait_ge(qk_ready, 2 * c + j + 1)
                    wait(act, split, 2 * c * 5 - 5 * (1 - j))
                    nc.scalar.activation(proj[:, j], psum[:, 1 + j, :], ACT.Identity, bias=bias,
                                         scale=scale).then_inc(qk_copied, 1)

            def gate(c):
                act.wait_ge(pick, c * PICK + SHIFTED)
                nc.scalar.activation(expd[:, :, :], shifted[:, :, :], ACT.Exp).then_inc(exps, 1)
                nc.scalar.activation(egap[:, :], gap[:, :], ACT.Exp).then_inc(exps, 1)

            def copy_masked(c):
                wait(act, in_ready, 2 * NF * c)
                for j in range(2):
                    act.wait_ge(mt_ready, 2 * c + j + 1)
                    nc.scalar.activation(maskedT[:, j], psum[:, 3 + j, :], ACT.Copy).then_inc(mt_copied, 1)

            def body(c, par):
                for f in range(0, NF, 2):
                    for k in range(2):
                        act.wait_ge(in_ready, 2 * (c * NF + f) + k + 1)
                        wait(act, hid_ready, c * NF + f + k - 1)
                        nc.scalar.activation(relu[:, k, 0], psum[:, 6 + k, :], ACT.Relu,
                                             bias=bcol[:, BI + f + k:BI + f + k + 1]).then_inc(in1_used, 1)
                    for k in range(2):
                        act.wait_ge(in_ready, 2 * (c * NF + f) + k + 3)
                        nc.scalar.activation(relu[:, k, 1], psum[:, 6 + k, :], ACT.Relu,
                                             bias=bcol[:, BI + f + k:BI + f + k + 1]).then_inc(in2_used, 1)
                    if f == 0 and not beyond(c + 1):
                        gate(c + 1)
                if not beyond(c + 2):
                    copy_x(c + 2, par)
                if not beyond(c + 1):
                    copy_masked(c + 1)
                if not beyond(c + 2):
                    copy_qk(c + 2)

            copy_x(0, 0)
            copy_qk(0)
            copy_x(1, 1)
            gate(0)
            copy_qk(1)
            copy_masked(0)
            chunks(body, act, 2)

        @block.vector
        def _(dve):
            def copy_products(c, par):
                for n in range(CT):
                    dve.wait_ge(vx_ready, c * CT + n + 1)
                    bank = psum[:, 3 + n % 2]
                    nc.vector.tensor_tensor(
                        values[:, bass.ds((c // 2) * PAIRS, PAIRS), bass.ds((c % 2) * CT + n, 1)].rearrange(
                            "p u o a d -> p (u o) (a d)"),
                        bank[:, XV:XV + C].rearrange("p (u w) -> p u w", u=PAIRS),
                        brow[:, BV:BV + C].rearrange("p (u w) -> p u w", u=PAIRS), ALU.add)
                    nc.vector.tensor_tensor(logit[:, par, n], bank[:, XG:XG + E], brow[:, GB:GB + E], ALU.add)
                    if n == 0:
                        wait(dve, mask_ready, 2 * c - 2)
                    nc.vector.tensor_copy(xa[:, par, n], bank[:, XA:XA + C]).then_inc(vx_copied, 1)

            def split_qk(c):
                for j in range(2):
                    dve.wait_ge(qk_copied, 2 * c + j + 1)
                    k0 = 2 * 5 * c + 5 * j
                    wait(dve, parts_out[j], 16 * NC * c)
                    nc.vector.tensor_copy(parts[:, j, 0], proj[:, j]).then_inc(split, 1)
                    dve.wait_ge(split, k0 + 1)
                    nc.vector.tensor_tensor(res[:, j, 0], proj[:, j], parts[:, j, 0], ALU.subtract).then_inc(split, 1)
                    dve.wait_ge(split, k0 + 2)
                    nc.vector.tensor_copy(parts[:, j, 1], res[:, j, 0]).then_inc(split, 1)
                    dve.wait_ge(split, k0 + 3)
                    nc.vector.tensor_tensor(res[:, j, 1], res[:, j, 0], parts[:, j, 1], ALU.subtract).then_inc(split, 1)
                    dve.wait_ge(split, k0 + 4)
                    nc.vector.tensor_copy(parts[:, j, 2], res[:, j, 1]).then_inc(split, 1)

            def wide(a):
                return a.unsqueeze(2).to_broadcast([P, CT, E])

            def linker(c, step):
                def link(ins):
                    ins.then_inc(pick, 1)
                    step[0] += 1
                    dve.wait_ge(pick, c * PICK + step[0])
                return link

            def choose(c, par):
                step = [0]
                link = linker(c, step)

                wait(dve, mask_ready, 2 * c)
                dve.wait_ge(vx_copied, CT * (c + 1))
                link(nc.vector.tensor_reduce(top[:, 0], logit[:, par], AX_X, ALU.max))
                source = logit[:, par]
                for j in range(2):
                    link(nc.vector.tensor_tensor(below[:, :, :], source, wide(top[:, j]), ALU.is_lt))
                    link(nc.vector.scalar_tensor_tensor(
                        cand[:, :, :].rearrange("p n e -> p (n e)"), below[:, :, :].rearrange("p n e -> p (n e)"),
                        float(E), iota[:, :, :].rearrange("p n e -> p (n e)"), ALU.mult, ALU.add))
                    link(nc.vector.tensor_reduce(first[:, j], cand[:, :, :], AX_X, ALU.min))
                    link(nc.vector.tensor_tensor(hot[:, j], iota[:, :, :], wide(first[:, j]), ALU.is_equal))
                    if j == 0:
                        link(nc.vector.scalar_tensor_tensor(
                            rest[:, :, :].rearrange("p n e -> p (n e)"), hot[:, 0].rearrange("p n e -> p (n e)"),
                            -3e38, logit[:, par].rearrange("p n e -> p (n e)"), ALU.mult, ALU.add))
                        link(nc.vector.tensor_reduce(top[:, 1], rest[:, :, :], AX_X, ALU.max))
                        source = rest[:, :, :]
                link(nc.vector.tensor_tensor(swap[:, :, :], hot[:, 1], hot[:, 0], ALU.subtract))
                assert step[0] == SWAPPED
                link(nc.vector.tensor_tensor(shifted[:, :, :], logit[:, par], wide(top[:, 0]), ALU.subtract))
                link(nc.vector.tensor_tensor(gap[:, :], top[:, 1], top[:, 0], ALU.subtract))
                assert step[0] == SHIFTED

            def gate_sum(c, par):
                step = [SHIFTED]
                link = linker(c, step)
                dve.wait_ge(exps, 2 * c + 2)
                wait(dve, y_chain, 2 * (c - 1))
                link(nc.vector.tensor_reduce(esum[:, :], expd[:, :, :], AX_X, ALU.add))
                link(nc.vector.reciprocal(einv[:, :], esum[:, :]))
                link(nc.vector.tensor_scalar(etop[:, :], egap[:, :], 1.0, None, ALU.add))
                link(nc.vector.tensor_tensor(vsum[:, par], etop[:, :], einv[:, :], ALU.mult))
                assert step[0] == PICK

            def add_output(c, par):
                wait(dve, y_chain, 2 * c)
                dve.wait_ge(y_ready, c + 1)
                nc.vector.tensor_tensor(outb[:, :, :], psum[:, 5, :].rearrange("p (n d) -> p n d", n=CT),
                                        bo2[:, :].unsqueeze(1).to_broadcast([P, CT, C]), ALU.add).then_inc(y_chain, 1)
                dve.wait_ge(y_chain, 2 * c + 1)
                dve.wait_ge(res_ready, c + 1)
                for n in range(CT):
                    tile = acc[:, bass.ds(c * CT + n, 1), :].rearrange("p o d -> p (o d)")
                    last = nc.vector.scalar_tensor_tensor(tile, outb[:, n], vsum[:, par, n:n + 1], tile,
                                                          ALU.mult, ALU.add)
                last.then_inc(y_chain, 1)

            for c in range(2):
                copy_products(c, c)
                choose(c, c)
                split_qk(c)
                if c == 0:
                    gate_sum(c, c)

            def body(c, par):
                if not beyond(c + 1):
                    gate_sum(c + 1, 1 - par)
                if not beyond(c + 2):
                    copy_products(c + 2, par)
                    choose(c + 2, par)
                    split_qk(c + 2)
                add_output(c, par)
            chunks(body, dve, 2)
            dve.wait_ge(y_chain, 2 * CHUNKS)

        @block.sync
        def _(sp):
            def store(c, par):
                for j, (dst, combos) in enumerate(((q_parts, COMBOS_Q), (k_parts, COMBOS_K))):
                    view = dst.rearrange("(b u) a c d t -> b c (u a) d t", b=B)
                    sp.wait_ge(split, 10 * c + 5 * j + 5)
                    for m, part in enumerate(combos):
                        sp.dma_start(
                            view[bass.ds(c // 2, 1), m, :, :, bass.ds((c % 2) * CHUNK, CHUNK)].rearrange(
                                "o g d t -> (o g) d t"),
                            parts[:, j, part]).then_inc(parts_out[j], 16)
            with sp.Fori(0, CHUNKS) as c:
                store(c, 0)
            for j in range(2):
                sp.wait_ge(parts_out[j], 16 * NC * CHUNKS)


def phase2(nc, sem, psum, values, heads_out, ident, ident_b, k_stage, k_blank, q_parts, k_parts,
           q_rows, k_rows, const_rows, factors):
    with ExitStack() as ph:
        def tmp(name, shape, dt=F32):
            return ph.enter_context(nc.sbuf_tensor(name, shape, dt))

        q_stage = tmp("q_stage", [P, RING, T], BF16)
        v_stage = tmp("v_stage", [P, RING, NT, 2, VP])
        probs = tmp("probs", [P, PROBS, 2, CHUNK])
        factor = tmp("factor", [P, RING, 2, P])
        negmax = tmp("negmax", [P, RING, 2, NT, 2])
        m_min = tmp("m_min", [P, 2, NT])
        m_rest = tmp("m_rest", [P, 2, 2, NT])
        m_pad = tmp("m_pad", [P, P], BF16)
        m_parts = m_pad[:, 0:6 * NT].rearrange("p (a k n) -> p a k n", a=2, k=3)
        nought = tmp("nought", [P, 2, NT])
        m_rows = tmp("m_rows", [2 * 3 * NT, P], BF16)
        y_cols = tmp("y_cols", [P, CHUNK])
        y_inv = tmp("y_inv", [P, CT, 4])

        fixed = sem("fixed_rows_staged")
        staged = [sem(f"unit_staged{r}") for r in range(RING)]
        v_zero = sem("v_stage_blank")
        v_staged = sem("v_staged")
        half_ready = sem("max_scores_in_psum")
        half_used = sem("half_maxima")
        m_ready = sem("maxima_ready")
        m_chain = sem("maxima_parts_chain")
        mt_ready = sem("maxima_t_in_psum")
        mt_copied = sem("maxima_t_copied")
        m_staged = [sem(f"maxima_staged{r}") for r in range(RING)]
        s_ready = sem("scores_in_psum")
        e_ready = sem("exponentials")
        d_ready = sem("diagonal_done")
        pv_done = sem("weighted_values")
        y_copied = sem("y_copied")
        yt_ready = sem("y_t_in_psum")
        y_inverse = sem("y_inverse")
        y_done = sem("y_normalised")

        LOADS = 7
        TILE_STEPS = 2 * NT
        HALVES = 2 * NT * 2
        M_STEPS = 5
        Y_BANK, T_BANK = 6, 7
        y_ps = psum[:, Y_BANK]
        misc = psum[:, T_BANK]

        def number(t, v):
            return t * RING + v

        def slot_of(v):
            return v % RING

        def fill(t, v):
            return t + (v // RING + 1)

        def beyond(t, v):
            return isinstance(t, int) and v >= UNITS

        def units(body, eng):
            body(0, 0)
            body(0, 1)
            with eng.Fori(0, (UNITS - 5) // RING) as t:
                for v in range(2, RING + 2):
                    body(t, v)
            for v in range(UNITS - 3, UNITS):
                body(0, v)

        with nc.Block() as block:
            @block.sync
            def _(sp):
                bits = const_rows.bitcast(BF16)
                q_bias, k_bias = q_rows.bitcast(BF16), k_rows.bitcast(BF16)

                def products(a):
                    return slice(a * QK, (a + 1) * QK)

                def most(a):
                    return slice(2 * QK + a * MX, 2 * QK + (a + 1) * MX)

                def bias(a):
                    return slice(MAIN + a * BR, MAIN + (a + 1) * BR)

                sp.wait_ge(k_blank, 1)
                for slot in range(RING):
                    for a in range(2):
                        sp.dma_start(q_stage[bias(a), slot], q_bias).then_inc(fixed, 16)
                        for form in range(2):
                            sp.dma_start(k_stage[most(a), slot, a, form], bits[0, 0:MX]).then_inc(fixed, 16)

                def stage(t, v):
                    u, slot = number(t, v), slot_of(v)
                    wait(sp, pv_done, (u - RING + 1) * NT)
                    sp.dma_start(factor[:, slot],
                                 factors[bass.ds(u % PAIRS, 1)].rearrange("o p a t -> (o p) a t")).then_inc(staged[slot], 16)
                    sp.dma_start(q_stage[0:2 * QK, slot],
                                 q_parts[bass.ds(u, 1)].rearrange("o a c d t -> (o a c d) t")).then_inc(staged[slot], 16)
                    sp.dma_start(q_stage[2 * QK:MAIN, slot], bits[1]).then_inc(staged[slot], 16)
                    for a in range(2):
                        sp.dma_start(
                            k_stage[products(a), slot, a],
                            k_parts[bass.ds(u, 1), a].rearrange("o c d t -> (o c d) t").unsqueeze(1).to_broadcast(
                                [QK, 2, T])).then_inc(staged[slot], 16)
                        sp.dma_start(
                            k_stage[bias(a), slot, a],
                            k_bias[bass.ds(u % PAIRS, 1), a].rearrange("o r f t -> (o r) f t")).then_inc(staged[slot], 16)

                def stage_maxima(t, v):
                    u, slot = number(t, v), slot_of(v)
                    wait(sp, mt_copied, u + 1)
                    sp.dma_start(q_stage[2 * QK:MAIN, slot, :], m_rows[:, :]).then_inc(m_staged[slot], 16)

                stage(0, 0)
                stage(0, 1)
                stage_maxima(0, 0)

                def body(t, v):
                    if not beyond(t, v + 2):
                        stage(t, v + 2)
                    if not beyond(t, v + 1):
                        stage_maxima(t, v + 1)
                units(body, sp)

            @block.gpsimd
            def _(pool):
                nc.gpsimd.memset(v_stage[:, :, :, :, :], 0.0).then_inc(v_zero, 1)
                pool.wait_ge(v_zero, 1)
                nc.gpsimd.memset(v_stage[:, :, :, :, D:D + 1], 1.0).then_inc(v_zero, 1)
                nc.gpsimd.memset(m_pad[:, :], 0.0).then_inc(v_zero, 1)
                nc.gpsimd.memset(nought[:, :, :], 0.0).then_inc(v_zero, 1)
                pool.wait_ge(v_zero, 4)

                def stage_values(t, v):
                    u, slot = number(t, v), slot_of(v)
                    wait(pool, pv_done, (u - RING + 1) * NT)
                    nc.gpsimd.tensor_copy(
                        v_stage[:, slot, :, :, 0:D].rearrange("p n a d -> p (n a) d"),
                        values[:, bass.ds(u, 1)].rearrange("p o n a d -> p (o n a) d")).then_inc(v_staged, 1)

                def maxima(t, v):
                    u, slot = number(t, v), slot_of(v)
                    k = [0]

                    def link(ins):
                        ins.then_inc(m_chain, 1)
                        k[0] += 1
                        wait(pool, m_chain, u * M_STEPS + k[0])

                    wait(pool, m_ready, u + 1)
                    wait(pool, mt_ready, u)
                    link(nc.gpsimd.tensor_tensor(m_parts[:, :, 0], m_min[:, :, :], nought[:, :, :], ALU.add))
                    link(nc.gpsimd.tensor_tensor(m_rest[:, 0], m_min[:, :, :], m_parts[:, :, 0], ALU.subtract))
                    link(nc.gpsimd.tensor_tensor(m_parts[:, :, 1], m_rest[:, 0], nought[:, :, :], ALU.add))
                    link(nc.gpsimd.tensor_tensor(m_rest[:, 1], m_rest[:, 0], m_parts[:, :, 1], ALU.subtract))
                    link(nc.gpsimd.tensor_tensor(m_parts[:, :, 2], m_rest[:, 1], nought[:, :, :], ALU.add))

                stage_values(0, 0)
                stage_values(0, 1)
                maxima(0, 0)

                def body(t, v):
                    u, slot = number(t, v), slot_of(v)
                    for i in range(NT):
                        c = i // CT
                        wait(pool, e_ready, u * TILE_STEPS + 2 * i + c + 1)
                        tile = probs[:, (2 * i + c) % PROBS, :, (i % CT) * P:(i % CT + 1) * P]
                        nc.gpsimd.tensor_tensor(
                            tile, tile,
                            factor[:, slot],
                            ALU.mult).then_inc(d_ready, 1)
                        if i == 1 and not beyond(t, v + 2):
                            stage_values(t, v + 2)
                        if i == NT // 2 and not beyond(t, v + 1):
                            maxima(t, v + 1)
                units(body, pool)

            @block.tensor
            def _(pe):
                def max_half(t, v, a, j, h):
                    u, slot = number(t, v), slot_of(v)
                    if j == 0 and a == 0 and h == 0:
                        pe.wait_ge(staged[slot], fill(t, v) * (LOADS * 16))
                    m = u * HALVES + (a * NT + j) * 2 + h
                    wait(pe, half_used, m - 1)
                    for s0, s1, form, rows in regions_by_keys(j, h):
                        ins = nc.tensor.matmul(
                            psum[:, 4 + h, s0 - h * 512:s1 - h * 512],
                            q_stage[0:rows, slot, j * P:(j + 1) * P],
                            k_stage[0:rows, slot, a, form, s0:s1], start=True, stop=True)
                    ins.then_inc(half_ready, 1)

                def scores(t, v, i, c, a):
                    u, slot = number(t, v), slot_of(v)
                    n = 2 * i + c
                    if n == 0 and a == 0:
                        pe.wait_ge(m_staged[slot], fill(t, v) * 16)
                    if a == 0:
                        wait(pe, e_ready, u * TILE_STEPS + n - 1)
                    for t0, t1, form, rows in regions_by_queries(i, c):
                        ins = nc.tensor.matmul(
                            psum[:, 2 * c + a, t0 - c * 512:t1 - c * 512],
                            k_stage[0:rows, slot, a, form, i * P:(i + 1) * P],
                            q_stage[0:rows, slot, t0:t1], start=True, stop=True)
                    if a == 1:
                        ins.then_inc(s_ready, 1)

                def weigh(t, v, i, part):
                    u, slot = number(t, v), slot_of(v)
                    qs = slice(part * CHUNK // 2, (part + 1) * CHUNK // 2)
                    if i == 0 and part == 0:
                        pe.wait_ge(v_staged, u + 1)
                        wait(pe, y_copied, u)
                    pe.wait_ge(e_ready, u * TILE_STEPS + 2 * i + 2)
                    pe.wait_ge(d_ready, u * NT + i + 1)
                    for a in range(2):
                        for c in range(2):
                            g = 32 * (2 * a + c)
                            ins = nc.tensor.matmul(y_ps[g:g + VP, qs], v_stage[:, slot, i, a, :],
                                                   probs[:, (2 * i + c) % PROBS, a, qs],
                                                   start=(i == 0 and part == 0), stop=(i == NT - 1),
                                                   skip_group_check=True)
                    if part == 1:
                        ins.then_inc(pv_done, 1)

                def turn_y(t, v):
                    u = number(t, v)
                    pe.wait_ge(y_copied, u + 1)
                    wait(pe, y_done, 2 * u)
                    pe.wait_ge(mt_copied, UNITS if beyond(t, v + 1) else u + 2)
                    for q in range(CT):
                        ins = nc.tensor.transpose(misc[:, q * P:(q + 1) * P], y_cols[:, q * P:(q + 1) * P], ident[:, :])
                    ins.then_inc(yt_ready, 1)

                def turn_maxima(t, v):
                    u = number(t, v)
                    wait(pe, y_done, 2 * (u - 1))
                    pe.wait_ge(m_chain, (u + 1) * M_STEPS)
                    nc.tensor.transpose(misc.bitcast(BF16)[:, 0:P], m_pad[:, :],
                                        ident_b[:, :]).then_inc(mt_ready, 1)

                pe.wait_ge(fixed, 16 * RING * 6)
                for v, a in ((0, 0), (0, 1), (1, 0)):
                    for j in range(NT):
                        for h in range(2):
                            max_half(0, v, a, j, h)
                turn_maxima(0, 0)

                def body(t, v):
                    start = isinstance(t, int) and v == 0
                    for i in range(NT):
                        def max_part(k):
                            j, h = 2 * (i % CT) + k // 2, k % 2
                            if i < CT and not beyond(t, v + 1):
                                max_half(t, v + 1, 1, j, h)
                            if i >= CT and not beyond(t, v + 2):
                                max_half(t, v + 2, 0, j, h)

                        for part in range(2):
                            max_part(2 * part)
                            if i >= LAG:
                                weigh(t, v, i - LAG, part)
                            elif not start:
                                weigh(t, v - 1, NT + i - LAG, part)
                            max_part(2 * part + 1)
                            for a in range(2):
                                scores(t, v, i, part, a)
                        if i == 4 and not start:
                            turn_y(t, v - 1)
                        if i == 6 and not beyond(t, v + 1):
                            turn_maxima(t, v + 1)
                units(body, pe)
                for i in range(NT - LAG, NT):
                    for part in range(2):
                        weigh(0, UNITS - 1, i, part)
                turn_y(0, UNITS - 1)

            @block.scalar
            def _(act):
                def copy_y(t, v):
                    u = number(t, v)
                    act.wait_ge(pv_done, (u + 1) * NT)
                    wait(act, yt_ready, u)
                    nc.scalar.activation(y_cols[:, :], y_ps, ACT.Copy).then_inc(y_copied, 1)

                def copy_maxima(t, v):
                    u = number(t, v)
                    act.wait_ge(mt_ready, u + 1)
                    if not (isinstance(t, int) and v == 0):
                        act.wait_ge(m_staged[slot_of(v - 1)], fill(t, v - 1) * 16)
                    nc.scalar.activation(m_rows[:, :], misc.bitcast(BF16)[0:48, 0:P], ACT.Copy).then_inc(mt_copied, 1)

                copy_maxima(0, 0)

                def body(t, v):
                    u = number(t, v)
                    for i in range(NT):
                        for c in range(2):
                            n = 2 * i + c
                            act.wait_ge(s_ready, u * TILE_STEPS + n + 1)
                            wait(act, pv_done, u * NT + i + 1 - PROBS // 2)
                            nc.scalar.activation(
                                probs[:, n % PROBS], psum[:, 2 * c:2 * c + 2, :], ACT.Exp).then_inc(e_ready, 1)
                            if n == 2 and not (isinstance(t, int) and v == 0):
                                copy_y(t, v - 1)
                        if i == 6 and not beyond(t, v + 1):
                            copy_maxima(t, v + 1)
                units(body, act)
                copy_y(0, UNITS - 1)

            @block.vector
            def _(dve):
                def reduce(t, v, a, j):
                    u, slot = number(t, v), slot_of(v)
                    for h in range(2):
                        dve.wait_ge(half_ready, u * HALVES + (a * NT + j) * 2 + h + 1)
                        nc.vector.tensor_reduce(negmax[:, slot, a, j, h:h + 1], psum[:, 4 + h, :], AX_X, ALU.max,
                                                negate=True).then_inc(half_used, 1)
                    if a == 1 and j == NT - 1:
                        dve.wait_ge(half_used, (u + 1) * HALVES)
                        wait(dve, m_chain, u * M_STEPS)
                        nc.vector.tensor_tensor(m_min[:, :, :], negmax[:, slot, :, :, 0], negmax[:, slot, :, :, 1],
                                                ALU.min).then_inc(m_ready, 1)

                def norm_y(t, v):
                    u = number(t, v)
                    wait(dve, y_done, 2 * u)
                    dve.wait_ge(yt_ready, u + 1)
                    grid = misc.rearrange("p (q g w) -> p q g w", q=CT, g=4)
                    nc.vector.reciprocal(y_inv[:, :, :], grid[:, :, :, D]).then_inc(y_inverse, 1)
                    dve.wait_ge(y_inverse, u + 1)
                    for a in range(2):
                        for c in range(2):
                            dst = heads_out[:, bass.ds(u, 1), c * CT:(c + 1) * CT, a * D:(a + 1) * D]
                            ins = nc.vector.tensor_tensor(
                                dst.rearrange("p o n d -> p (o n) d"), grid[:, :, 2 * a + c, 0:D],
                                y_inv[:, :, 2 * a + c].unsqueeze(2).to_broadcast([P, CT, D]), ALU.mult)
                        ins.then_inc(y_done, 1)

                for j in range(NT):
                    reduce(0, 0, 0, j)
                for j in range(NT):
                    reduce(0, 0, 1, j)
                for j in range(NT):
                    reduce(0, 1, 0, j)

                def body(t, v):
                    for i in range(NT):
                        for j in range(2 * (i % CT), 2 * (i % CT) + 2):
                            if i < CT and not beyond(t, v + 1):
                                reduce(t, v + 1, 1, j)
                            if i >= CT and not beyond(t, v + 2):
                                reduce(t, v + 2, 0, j)
                        if i == 4 and not (isinstance(t, int) and v == 0):
                            norm_y(t, v - 1)
                units(body, dve)
                norm_y(0, UNITS - 1)
                dve.wait_ge(y_done, 2 * UNITS)


def regions_by_keys(j, h):
    lo, hi = h * 512, h * 512 + 512
    spans = ((0, j * P, 1, ALL), (j * P, (j + 1) * P, 0, ALL), ((j + 1) * P, T, 0, MAIN))
    return [(max(lo, s0), min(hi, s1), form, rows) for s0, s1, form, rows in spans if max(lo, s0) < min(hi, s1)]


def regions_by_queries(i, c):
    lo, hi = c * 512, c * 512 + 512
    spans = ((0, i * P, 0, MAIN), (i * P, (i + 1) * P, 0, ALL), ((i + 1) * P, T, 1, ALL))
    return [(max(lo, t0), min(hi, t1), form, rows) for t0, t1, form, rows in spans if max(lo, t0) < min(hi, t1)]


def phase3(nc, sem, psum, acc, heads_out, ident, wp, out):
    with ExitStack() as ph:
        gathered = ph.enter_context(nc.sbuf_tensor("gathered", [P, 2, CT, C], F32))
        turned = ph.enter_context(nc.sbuf_tensor("turned", [P, 2, CHUNK], F32))
        g_ready = sem("gathered_ready")
        t_ready = sem("turned_in_psum")
        t_copied = sem("turned_copied")
        p_ready = sem("projected")
        p_added = sem("projection_added")
        stored = sem("stored")
        out_v = out.rearrange("b (n p) d -> p (b n) d", p=P)

        with nc.Block() as block:
            @block.gpsimd
            def _(pool):
                def body(c, par):
                    wait(pool, t_ready, c - 1)
                    nc.gpsimd.tensor_copy(
                        gathered[:, par].rearrange("p n (u w) -> p n u w", u=PAIRS),
                        heads_out[:, bass.ds((c // 2) * PAIRS, PAIRS), par * CT:(par + 1) * CT].rearrange(
                            "p u n w -> p n u w")).then_inc(g_ready, 1)
                chunks(body, pool, 2)

            @block.tensor
            def _(pe):
                def turn(c, par):
                    pe.wait_ge(g_ready, c + 1)
                    wait(pe, t_copied, c - 1)
                    for n in range(CT):
                        ins = nc.tensor.transpose(psum[:, par, n * P:(n + 1) * P], gathered[:, par, n], ident[:, :])
                    ins.then_inc(t_ready, 1)

                turn(0, 0)

                def body(c, par):
                    if not (isinstance(c, int) and c == CHUNKS - 1):
                        turn(c + 1, 1 - par)
                    pe.wait_ge(t_copied, c + 1)
                    wait(pe, p_added, c - 1)
                    for n in range(CT):
                        ins = nc.tensor.matmul(psum[:, 2 + par, n * P:(n + 1) * P], turned[:, par, n * P:(n + 1) * P],
                                               wp[:, :], start=True, stop=True)
                    ins.then_inc(p_ready, 1)
                chunks(body, pe, 2)

            @block.scalar
            def _(act):
                def body(c, par):
                    act.wait_ge(t_ready, c + 1)
                    wait(act, p_ready, c - 1)
                    nc.scalar.activation(turned[:, par], psum[:, par], ACT.Copy).then_inc(t_copied, 1)
                chunks(body, act, 2)

            @block.vector
            def _(dve):
                def body(c, par):
                    dve.wait_ge(p_ready, c + 1)
                    tiles = acc[:, bass.ds(c * CT, CT), :].rearrange("p n d -> p (n d)")
                    nc.vector.tensor_tensor(tiles, psum[:, 2 + par], tiles, ALU.add).then_inc(p_added, 1)
                chunks(body, dve, 2)

            @block.sync
            def _(sp):
                def body(c, par):
                    sp.wait_ge(p_added, c + 1)
                    sp.dma_start(out_v[:, bass.ds(c * CT, CT), :], acc[:, bass.ds(c * CT, CT), :]).then_inc(stored, 16)
                chunks(body, sp, 2)
                sp.wait_ge(stored, 16 * CHUNKS)


def rounded(v):
    bits = np.asarray(v, np.float32).view(np.uint32)
    return ((bits + 0x7FFF + ((bits >> 16) & 1)) & 0xFFFF0000).astype(np.uint32).view(np.float32)


def constants():
    def parts3(v):
        v = np.asarray(v, np.float32)
        a = rounded(v)
        b = rounded(v - a)
        return a, b, rounded(v - a - b)

    def bits(v):
        return (rounded(v).view(np.uint32) >> 16).astype(np.uint16)

    start = 2.0 ** (-2.0 ** (-(np.log2(H) - 3)))
    slopes = np.array([start * start ** i for i in range(H)]).astype(np.float32)
    pos = np.arange(T)
    lane = pos % P
    steps = range(1, P // STEP)
    q_rows = np.zeros((BR, T), np.float32)
    for m in steps:
        q_rows[m - 1] = lane >= m * STEP
    q_rows[3:6] = 1.0
    q_rows[6:9] = lane
    q_rows[9:12] = (pos // P - NT // 2) * P
    k_rows = np.zeros((H, BR, 2, T), np.float32)
    factors = np.zeros((P, H, P), np.float32)
    s_l, t_l = np.arange(P)[:, None], np.arange(P)[None, :]
    for h in range(H):
        step = rounded(slopes[h:h + 1] * np.float32(STEP))[0]
        for m in steps:
            k_rows[h, m - 1, 0] = np.where(lane < m * STEP, -step, 0.0)
        k_rows[h, 3:6, 1] = parts3(slopes[h] * (pos - T // 2).astype(np.float32))
        for p, part in enumerate(parts3(slopes[h:h + 1])):
            k_rows[h, 6 + p, 1] = -part[0]
            k_rows[h, 9 + p, 1] = -part[0]
        stairs = sum(((s_l < m * STEP) & (t_l >= m * STEP)).astype(np.float64) for m in steps)
        factors[:, h] = np.exp(float(slopes[h]) * np.minimum(s_l - t_l, 0) + float(step) * stairs)
    const_rows = np.stack([np.ones((2 * MX, T), np.float32), np.zeros((2 * MX, T), np.float32)])
    return dict(ident_in=np.eye(P, dtype=np.float32),
                iota_in=np.ascontiguousarray(np.broadcast_to(np.arange(E, dtype=np.float32), (P, CT, E))),
                q_rows=bits(q_rows), k_rows=bits(k_rows).reshape(PAIRS, 2, BR, 2, T),
                const_rows=bits(const_rows),
                factors=factors.reshape(P, PAIRS, 2, P).transpose(1, 0, 2, 3))


def kernel(L0_attn_x, L0_attn_W_qkv, L0_attn_b_qkv, L0_attn_W_proj, L0_attn_b_proj, L0_ffn_wi, L0_ffn_bi,
           L0_ffn_wo, L0_ffn_bo, L0_ffn_lora_A, L0_ffn_lora_B, L0_ffn_gate_w, L0_ffn_gate_b):
    import concourse.bacc as _bacc
    from concourse.bass_utils import run_bass_kernel_spmd as _run

    w_qkv, b_qkv = np.asarray(L0_attn_W_qkv), np.asarray(L0_attn_b_qkv)
    row = np.concatenate([b_qkv[2 * C:], np.asarray(L0_attn_b_proj), np.asarray(L0_ffn_bo),
                          np.asarray(L0_ffn_gate_b)])
    laid = dict(
        x=np.asarray(L0_attn_x),
        w_q=w_qkv[:, 0:C], w_k=w_qkv[:, C:2 * C],
        w_x=np.concatenate([w_qkv[:, 2 * C:], np.asarray(L0_ffn_lora_A).reshape(E * R, C).T,
                            np.asarray(L0_ffn_gate_w).T], axis=1),
        w_i=np.asarray(L0_ffn_wi).T,
        w_b=np.asarray(L0_ffn_lora_B).transpose(0, 2, 1).reshape(E * R, F),
        w_o=np.asarray(L0_ffn_wo).T.reshape(F // P, P, C).transpose(1, 0, 2),
        w_p=np.asarray(L0_attn_W_proj),
        bias_rows=np.broadcast_to(row, (P, row.shape[0])),
        bias_cols=np.concatenate([b_qkv[0:2 * C].reshape(2, C).T, np.asarray(L0_ffn_bi).reshape(F // P, P).T], axis=1),
    )
    laid.update(constants())
    nc = _bacc.Bacc("TRN2", target_bir_lowering=False, num_devices=1)
    arrays, args = {}, {}
    for name, a in laid.items():
        a = np.ascontiguousarray(a)
        arrays[f"in_{name}"] = a
        args[name] = nc.dram_tensor(f"in_{name}", a.shape, mybir.dt.from_np(a.dtype), kind="ExternalInput").ap()
    args["out"] = nc.dram_tensor("out", (B, T, C), F32, kind="ExternalOutput").ap()
    build(nc, **args)
    r = _run(nc, [arrays], core_ids=[0])
    return r.results[0]["out"]
```

```python
from contextlib import ExitStack

import numpy as np

import concourse.bass as bass
from concourse import mybir

F32 = mybir.dt.float32
BF16 = mybir.dt.bfloat16
ALU = mybir.AluOpType
ACT = mybir.ActivationFunctionType
AX_X = mybir.AxisListType.X

P = 128
B, T, C, H, D = 4, 1024, 128, 16, 8
E, R, F = 8, 16, 512
NT = T // P
TILES = B * NT
CT = 4
CHUNK = CT * P
CHUNKS = TILES // CT
PAIRS = H // 2
UNITS = B * PAIRS
COMBOS_Q = (0, 0, 1, 1, 0, 2)
COMBOS_K = (0, 1, 0, 1, 2, 0)
NC = len(COMBOS_Q)
QK = NC * D
MX = 3
BR = 12
MAIN = 2 * (QK + MX)
ALL = MAIN + 2 * BR
STEP = 32
RING = 3
PROBS = 8
LAG = 2
VP = 32
MAX_LINKS = 5
LOADS = 7
HALVES = 2 * NT * 2
EPS = 1e-5
SCALE = 1.0 / float(np.sqrt(D))
BV, BP, BO, GB = 0, C, 2 * C, 3 * C
BQ, BK, BI = 0, 1, 2
XV, XA, XG = 0, C, 2 * C
XW = 2 * C + E


FIRST_HALVES = [(v, a, j, h) for v, a in ((0, 0), (0, 1), (1, 0)) for j in range(NT) for h in range(2)]
FFN_STEPS = 3 * (F // P)
EARLY_HALVES = {CHUNKS - 2: [0] * 6 + [1] * (FFN_STEPS - 6) + [4] + [1] * CT,
                CHUNKS - 1: [1] * 2 + [2] * (FFN_STEPS - 2) + [4] + [2] * CT}
EARLY_SUM = sum(sum(v) for v in EARLY_HALVES.values())


def wait(eng, sem, value):
    if isinstance(value, int) and value <= 0:
        return
    eng.wait_ge(sem, value)


def chunks(body, eng, ends=1):
    for c in range(ends):
        body(c, c % 2)
    with eng.Fori(0, CHUNKS // 2 - ends) as t:
        for k in range(ends, ends + 2):
            body(t * 2 + k, k % 2)
    for c in range(CHUNKS - ends, CHUNKS):
        body(c, c % 2)


def build(nc, x, w_q, w_k, w_x, w_i, w_b, w_o, w_p, bias_rows, bias_cols, ident_in, iota_in,
          q_rows, k_rows, const_rows, factors, out):
    with ExitStack() as ctx:
        def sb(name, shape, dt=F32):
            return ctx.enter_context(nc.sbuf_tensor(name, shape, dt))

        def sem(name):
            return ctx.enter_context(nc.semaphore(name))

        q_parts = nc.dram_tensor("q_parts", (UNITS, 2, NC, D, T), BF16, kind="Internal").ap()
        k_parts = nc.dram_tensor("k_parts", (UNITS, 2, NC, D, T), BF16, kind="Internal").ap()

        acc = sb("acc", [P, TILES, C])
        values = sb("values", [P, UNITS, NT, 2, D])
        heads_out = sb("heads_out", [P, NT, B * C])
        brow = sb("brow", [P, 3 * C + E])
        bcol = sb("bcol", [P, 6])
        ident = sb("ident", [P, P])
        ident_b = sb("ident_b", [P, P], BF16)
        wp = sb("wp", [P, C])

        k_stage = sb("k_stage", [P, RING, 2, 2, T], BF16)
        q_stage = sb("q_stage", [P, RING, T], BF16)
        factor = sb("factor", [P, RING, 2, P])
        negmax = sb("negmax", [P, RING, 2, NT, 2])
        v_stage = sb("v_stage", [P, RING, NT, 2, VP])
        m_min = sb("m_min", [P, 2, NT])
        m_pad = sb("m_pad", [P, P], BF16)
        nought = sb("nought", [P, 2, NT])

        psum = ctx.enter_context(nc.psum_tensor("psum", [P, 8, 512], F32))

        k_blank = sem("k_stage_blank")
        v_zero = sem("v_stage_blank")
        steps = unit_steps(
            nc, sem, sb, psum, k_stage, q_stage, v_stage, factor, negmax, m_min, m_pad, nought, values, ident_b,
            k_blank, q_parts, k_parts, q_rows, k_rows, const_rows, factors)

        with ExitStack() as ph:
            def tmp(name, shape, dt=F32):
                return ph.enter_context(nc.sbuf_tensor(name, shape, dt))

            xc = tmp("xc", [P, TILES, C])
            wq = tmp("wq", [P, C])
            wk = tmp("wk", [P, C])
            wx = tmp("wx", [P, XW])
            wi = tmp("wi", [P, F])
            wb = tmp("wb", [P, F])
            wo = tmp("wo", [P, F // P, C])
            iota = tmp("iota", [P, CT, E])
            bqs = tmp("bqs", [P, 1])
            rstd = tmp("rstd", [P, TILES])
            bo2 = tmp("bo2", [P, C])
            sums = tmp("sums", [P, TILES])
            mean = tmp("mean", [P, TILES])
            ssq = tmp("ssq", [P, TILES])
            var = tmp("var", [P, TILES])
            root = tmp("root", [P, TILES])
            rinv = tmp("rinv", [P, TILES])
            quo = tmp("quo", [P, TILES])
            total = tmp("total", [P, TILES])
            root2 = tmp("root2", [P, TILES])

            s_x = [sem(f"x_loaded{b}") for b in range(B)]
            s_w = sem("weights_loaded")
            s_sum = sem("row_sums")
            s_mean = sem("means")
            s_xc = sem("centred")
            s_ssq = sem("squares_summed")
            s_chain = sem("variance_chain")
            s_root = sem("rooted")
            s_const = sem("constants_made")
            W_LOADS = 11
            LN_STEPS = 6
            GROUPS = (slice(0, NT), slice(NT, TILES))

            def centre(dve, b):
                g = slice(b * NT, (b + 1) * NT)
                dve.wait_ge(s_x[b], 16)
                nc.vector.tensor_reduce(sums[:, g], acc[:, g, :], AX_X, ALU.add).then_inc(s_sum, 1)
                dve.wait_ge(s_sum, b + 1)
                nc.vector.tensor_scalar(mean[:, g], sums[:, g], 1.0 / C, None, ALU.mult).then_inc(s_mean, 1)
                dve.wait_ge(s_mean, b + 1)
                nc.vector.tensor_tensor(
                    xc[:, g, :], acc[:, g, :], mean[:, g].unsqueeze(2).to_broadcast([P, NT, C]),
                    ALU.subtract).then_inc(s_xc, 1)

            def square(act, b):
                act.wait_ge(s_xc, b + 1)
                for n in range(b * NT, (b + 1) * NT):
                    nc.scalar.activation(heads_out[:, n % NT, b * C:(b + 1) * C], xc[:, n, :], ACT.Square,
                                         accum_out=ssq[:, n:n + 1]).then_inc(s_ssq, 1)

            def variance(dve, k):
                g = GROUPS[k]
                dve.wait_ge(s_ssq, g.stop)
                nc.vector.tensor_scalar(var[:, g], ssq[:, g], 1.0 / C, EPS, ALU.mult, ALU.add).then_inc(s_chain, 1)

            def root_of(act, k):
                act.wait_ge(s_chain, LN_STEPS * k + 1)
                nc.scalar.activation(root[:, GROUPS[k]], var[:, GROUPS[k]], ACT.Sqrt).then_inc(s_root, 1)

            def refine(dve, k):
                g, done = GROUPS[k], LN_STEPS * k + 1
                dve.wait_ge(s_root, k + 1)
                nc.vector.reciprocal(rinv[:, g], root[:, g]).then_inc(s_chain, 1)
                dve.wait_ge(s_chain, done + 1)
                nc.vector.tensor_tensor(quo[:, g], var[:, g], rinv[:, g], ALU.mult).then_inc(s_chain, 1)
                dve.wait_ge(s_chain, done + 2)
                nc.vector.tensor_tensor(total[:, g], quo[:, g], root[:, g], ALU.add).then_inc(s_chain, 1)
                dve.wait_ge(s_chain, done + 3)
                nc.vector.tensor_scalar(root2[:, g], total[:, g], 0.5, None, ALU.mult).then_inc(s_chain, 1)
                dve.wait_ge(s_chain, done + 4)
                nc.vector.reciprocal(rstd[:, g], root2[:, g]).then_inc(s_chain, 1)

            def wait_norms(eng):
                eng.wait_ge(s_xc, B)
                eng.wait_ge(s_chain, LN_STEPS * len(GROUPS))

            def make_constants(dve):
                dve.wait_ge(s_w, 16 * W_LOADS)
                nc.vector.tensor_scalar(bqs[:, :], bcol[:, BQ:BQ + 1], SCALE, None, ALU.mult).then_inc(s_const, 1)
                nc.vector.tensor_copy(ident_b[:, :], ident[:, :]).then_inc(s_const, 1)
                nc.vector.tensor_scalar(bo2[:, :], brow[:, BO:BO + C], 2.0, None, ALU.mult).then_inc(s_const, 1)

            def wait_weights(eng):
                eng.wait_ge(s_w, 16 * W_LOADS)

            def wait_constants(eng):
                eng.wait_ge(s_const, 4)

            def blank_values(pool):
                nc.gpsimd.memset(v_stage[:, :, :, :, :], 0.0).then_inc(v_zero, 1)
                pool.wait_ge(v_zero, 1)
                nc.gpsimd.memset(v_stage[:, :, :, :, D:D + 1], 1.0).then_inc(v_zero, 1)
                nc.gpsimd.memset(m_pad[:, :], 0.0).then_inc(v_zero, 1)
                nc.gpsimd.memset(nought[:, :, :], 0.0).then_inc(v_zero, 1)
                pool.wait_ge(v_zero, 4)

            norms = Steps()
            norms.blank_values = blank_values
            norms.make_constants, norms.wait_constants = make_constants, wait_constants
            norms.wait_weights = wait_weights
            norms.centre, norms.square, norms.variance, norms.root_of = centre, square, variance, root_of
            norms.refine, norms.wait = refine, wait_norms

            with nc.Block() as block:
                x_v = x.rearrange("b (n p) d -> b p n d", p=P)

                @block.sync
                def _(sp):
                    for b in range(B):
                        sp.dma_start(acc[:, b * NT:(b + 1) * NT, :], x_v[b]).then_inc(s_x[b], 16)
                    for dst, src in ((wq, w_q), (wk, w_k), (wx, w_x), (wi, w_i), (wb, w_b), (wp, w_p),
                                     (brow, bias_rows), (bcol, bias_cols), (ident, ident_in)):
                        sp.dma_start(dst[:, :], src).then_inc(s_w, 16)
                    sp.dma_start(wo[:, :, :], w_o).then_inc(s_w, 16)
                    sp.dma_start(iota[:, :, :], iota_in).then_inc(s_w, 16)

                @block.gpsimd
                def _(pool):
                    nc.gpsimd.memset(k_stage[:, :, :, :, :], 0.0).then_inc(k_blank, 1)

                @block.vector
                def _(dve):
                    nc.vector.memset(total[:, 0:1], 1.0).then_inc(s_const, 1)
                    centre(dve, 0)
                    variance(dve, 0)
                    refine(dve, 0)

                @block.scalar
                def _(act):
                    act.wait_ge(s_const, 1)
                    nc.scalar.activation(rinv[:, 0:1], total[:, 0:1], ACT.Sqrt)
                    square(act, 0)
                    root_of(act, 0)

            phase1(nc, ph, sem, psum, acc, values, brow, bcol, ident, xc, wq, wk, wx, wi, wb, wo, iota,
                   bqs, bo2, rstd, norms, q_parts, k_parts, steps)
        phase2(nc, sem, psum, values, heads_out, ident, ident_b, k_stage, q_stage, v_stage, factor,
               acc, wp, out, steps)


class Steps:
    pass


def number(t, v):
    return t * RING + v


def slot_of(v):
    return v % RING


def fill(t, v):
    return t + (v // RING + 1)


def unit_steps(nc, sem, sb, psum, k_stage, q_stage, v_stage, factor, negmax, m_min, m_pad, nought, values, ident_b,
               k_blank, q_parts, k_parts, q_rows, k_rows, const_rows, factors):
    fixed = sem("fixed_rows_staged")
    staged = [sem(f"unit_staged{r}") for r in range(RING)]
    half_ready = sem("max_scores_in_psum")
    half_used = sem("half_maxima")
    m_ready = sem("maxima_ready")
    m_chain = sem("maxima_parts_chain")
    mt_ready = sem("maxima_t_in_psum")
    mt_copied = sem("maxima_t_copied")
    m_staged = [sem(f"maxima_staged{r}") for r in range(RING)]
    v_staged = sem("v_staged")
    pv_done = sem("weighted_values")
    yt_copied = sem("y_t_copied")
    m_rows = sb("m_rows", [2 * 3 * NT, P], BF16)
    m_rest = sb("m_rest", [P, 2, 2, NT])
    m_parts = m_pad[:, 0:6 * NT].rearrange("p (a k n) -> p a k n", a=2, k=3)
    bits = const_rows.bitcast(BF16)
    q_bias, k_bias = q_rows.bitcast(BF16), k_rows.bitcast(BF16)

    def products(a):
        return slice(a * QK, (a + 1) * QK)

    def most(a):
        return slice(2 * QK + a * MX, 2 * QK + (a + 1) * MX)

    def bias(a):
        return slice(MAIN + a * BR, MAIN + (a + 1) * BR)

    def stage_fixed(sp):
        sp.wait_ge(k_blank, 1)
        for slot in range(RING):
            for a in range(2):
                sp.dma_start(q_stage[bias(a), slot], q_bias).then_inc(fixed, 16)
                for form in range(2):
                    sp.dma_start(k_stage[most(a), slot, a, form], bits[0, 0:MX]).then_inc(fixed, 16)

    def stage(sp, t, v):
        u, slot = number(t, v), slot_of(v)
        wait(sp, pv_done, (u - RING + 1) * NT)
        sp.dma_start(factor[:, slot],
                     factors[bass.ds(u % PAIRS, 1)].rearrange("o p a t -> (o p) a t")).then_inc(staged[slot], 16)
        sp.dma_start(q_stage[0:2 * QK, slot],
                     q_parts[bass.ds(u, 1)].rearrange("o a c d t -> (o a c d) t")).then_inc(staged[slot], 16)
        sp.dma_start(q_stage[2 * QK:MAIN, slot], bits[1]).then_inc(staged[slot], 16)
        for a in range(2):
            sp.dma_start(
                k_stage[products(a), slot, a],
                k_parts[bass.ds(u, 1), a].rearrange("o c d t -> (o c d) t").unsqueeze(1).to_broadcast(
                    [QK, 2, T])).then_inc(staged[slot], 16)
            sp.dma_start(
                k_stage[bias(a), slot, a],
                k_bias[bass.ds(u % PAIRS, 1), a].rearrange("o r f t -> (o r) f t")).then_inc(staged[slot], 16)

    def max_half(pe, t, v, a, j, h, bank):
        u, slot = number(t, v), slot_of(v)
        if j == 0 and a == 0 and h == 0:
            pe.wait_ge(staged[slot], fill(t, v) * (LOADS * 16))
        if isinstance(u, int) and u == 0 and a == 0 and j == 0 and h == 0:
            pe.wait_ge(fixed, 16 * RING * 6)
        for s0, s1, form, rows in regions_by_keys(j, h):
            ins = nc.tensor.matmul(
                psum[:, bank, s0 - h * 512:s1 - h * 512],
                q_stage[0:rows, slot, j * P:(j + 1) * P],
                k_stage[0:rows, slot, a, form, s0:s1], start=True, stop=True)
        ins.then_inc(half_ready, 1)

    def first_half(pe, v, a, j, h, bank):
        wait(pe, half_used, v * HALVES + (a * NT + j) * 2 + h - 1)
        max_half(pe, 0, v, a, j, h, bank + h)

    def reduce_half(dve, t, v, a, j, h, bank):
        u, slot = number(t, v), slot_of(v)
        dve.wait_ge(half_ready, u * HALVES + (a * NT + j) * 2 + h + 1)
        nc.vector.tensor_reduce(negmax[:, slot, a, j, h:h + 1], psum[:, bank, :], AX_X, ALU.max,
                                negate=True).then_inc(half_used, 1)
        if a == 1 and j == NT - 1 and h == 1:
            dve.wait_ge(half_used, (u + 1) * HALVES)
            wait(dve, m_chain, u * MAX_LINKS)
            nc.vector.tensor_tensor(m_min[:, :, :], negmax[:, slot, :, :, 0], negmax[:, slot, :, :, 1],
                                    ALU.min).then_inc(m_ready, 1)

    def stage_maxima(sp, t, v):
        u, slot = number(t, v), slot_of(v)
        wait(sp, mt_copied, u + 1)
        sp.dma_start(q_stage[2 * QK:MAIN, slot, :], m_rows[:, :]).then_inc(m_staged[slot], 16)

    def stage_values(pool, t, v):
        u, slot = number(t, v), slot_of(v)
        wait(pool, pv_done, (u - RING + 1) * NT)
        nc.gpsimd.tensor_copy(
            v_stage[:, slot, :, :, 0:D].rearrange("p n a d -> p (n a) d"),
            values[:, bass.ds(u, 1)].rearrange("p o n a d -> p (o n a) d")).then_inc(v_staged, 1)

    def part_maxima(pool, t, v):
        u, slot = number(t, v), slot_of(v)
        k = [0]

        def link(ins):
            ins.then_inc(m_chain, 1)
            k[0] += 1
            wait(pool, m_chain, u * MAX_LINKS + k[0])

        wait(pool, m_ready, u + 1)
        wait(pool, mt_ready, u)
        link(nc.gpsimd.tensor_tensor(m_parts[:, :, 0], m_min[:, :, :], nought[:, :, :], ALU.add))
        link(nc.gpsimd.tensor_tensor(m_rest[:, 0], m_min[:, :, :], m_parts[:, :, 0], ALU.subtract))
        link(nc.gpsimd.tensor_tensor(m_parts[:, :, 1], m_rest[:, 0], nought[:, :, :], ALU.add))
        link(nc.gpsimd.tensor_tensor(m_rest[:, 1], m_rest[:, 0], m_parts[:, :, 1], ALU.subtract))
        link(nc.gpsimd.tensor_tensor(m_parts[:, :, 2], m_rest[:, 1], nought[:, :, :], ALU.add))

    def turn_maxima(pe, t, v, bank):
        u = number(t, v)
        pe.wait_ge(m_chain, (u + 1) * MAX_LINKS)
        nc.tensor.transpose(psum[:, bank].bitcast(BF16)[:, 0:P], m_pad[:, :],
                            ident_b[:, :]).then_inc(mt_ready, 1)

    def copy_maxima(act, t, v, bank):
        u = number(t, v)
        act.wait_ge(mt_ready, u + 1)
        if not (isinstance(t, int) and v == 0):
            act.wait_ge(m_staged[slot_of(v - 1)], fill(t, v - 1) * 16)
        nc.scalar.activation(m_rows[:, :], psum[:, bank].bitcast(BF16)[0:2 * 3 * NT, 0:P], ACT.Copy).then_inc(mt_copied, 1)

    steps = Steps()
    steps.stage_fixed, steps.stage = stage_fixed, stage
    steps.stage_maxima, steps.stage_values = stage_maxima, stage_values
    steps.max_half, steps.first_half, steps.reduce_half = max_half, first_half, reduce_half
    steps.part_maxima, steps.half_used = part_maxima, half_used
    steps.turn_maxima, steps.copy_maxima = turn_maxima, copy_maxima
    steps.m_staged, steps.v_staged, steps.mt_copied = m_staged, v_staged, mt_copied
    steps.pv_done, steps.yt_copied = pv_done, yt_copied
    return steps


def phase1(nc, ph, sem, psum, acc, values, brow, bcol, ident, xc, wq, wk, wx, wi, wb, wo, iota,
           bqs, bo2, rstd, norms, q_parts, k_parts, steps):
    def tmp(name, shape, dt=F32):
        return ph.enter_context(nc.sbuf_tensor(name, shape, dt))

    xn = tmp("xn", [P, 2, CT, C])
    xnT = tmp("xnT", [P, 2, CHUNK])
    proj = tmp("proj", [P, 2, 2, CHUNK])
    res = tmp("res", [P, 2, 2, CHUNK])
    parts = tmp("parts", [P, 2, 3, CHUNK], BF16)
    xa = tmp("xa", [P, 2, CT, C])
    logit = tmp("logit", [P, 2, CT, E])
    top = tmp("top", [P, 2, CT])
    below = tmp("below", [P, CT, E])
    cand = tmp("cand", [P, CT, E])
    first = tmp("first", [P, 2, CT])
    hot = tmp("hot", [P, 2, CT, E])
    swap = tmp("swap", [P, CT, E])
    rest = tmp("rest", [P, CT, E])
    shifted = tmp("shifted", [P, CT, E])
    expd = tmp("expd", [P, CT, E])
    esum = tmp("esum", [P, CT])
    einv = tmp("einv", [P, CT])
    etop = tmp("etop", [P, CT])
    vsum = tmp("vsum", [P, 2, CT])
    gap = tmp("gap", [P, CT])
    egap = tmp("egap", [P, CT])
    masked = tmp("masked", [P, 2, CT, C])
    maskedT = tmp("maskedT", [P, 2, CHUNK])
    relu = tmp("relu", [P, 2, 2, CHUNK])
    hid = tmp("hid", [P, F // P, CHUNK])
    outb = tmp("outb", [P, CT, C])

    xn_ready = sem("xn_ready")
    res_ready = sem("residual_ready")
    xt_ready = sem("xt_in_psum")
    xt_copied = sem("xt_copied")
    qk_ready = sem("qk_in_psum")
    qk_copied = sem("qk_copied")
    vx_ready = sem("vx_in_psum")
    vx_copied = sem("vx_copied")
    split = sem("split_chain")
    parts_out = [sem("q_parts_stored"), sem("k_parts_stored")]
    pick = sem("pick_chain")
    exps = sem("gate_exps")
    mask_ready = sem("masked_ready")
    mt_ready = sem("masked_t_in_psum")
    mt_copied = sem("masked_t_copied")
    in_ready = sem("inter_in_psum")
    in1_used = sem("first_relu")
    in2_used = sem("second_relu")
    hid_ready = sem("hidden_ready")
    y_ready = sem("ffn_in_psum")
    y_chain = sem("ffn_out_chain")
    NF = F // P
    VX_BANKS = (3, 4, 0, 3)
    SWAPPED, SHIFTED = 12, 14
    PICK = 18

    def beyond(c):
        return isinstance(c, int) and c >= CHUNKS

    def early(c):
        return isinstance(c, int) and c in EARLY_HALVES

    with nc.Block() as block:
        @block.gpsimd
        def _(pool):
            def norm(c, par):
                wait(pool, xt_ready, c - 1)
                if isinstance(c, int) and c == NT // CT:
                    norms.wait(pool)
                nc.gpsimd.tensor_tensor(
                    xn[:, par], xc[:, bass.ds(c * CT, CT), :],
                    rstd[:, bass.ds(c * CT, CT)].unsqueeze(2).to_broadcast([P, CT, C]), ALU.mult).then_inc(xn_ready, 1)

            def residual(c):
                nc.gpsimd.tensor_tensor(
                    acc[:, bass.ds(c * CT, CT), :], acc[:, bass.ds(c * CT, CT), :],
                    brow[:, BP:BP + C].unsqueeze(1).to_broadcast([P, CT, C]), ALU.add).then_inc(res_ready, 1)

            def mask(c, par):
                wait(pool, vx_copied, (c + 1) * CT)
                wait(pool, pick, c * PICK + SWAPPED)
                wait(pool, mt_ready, 2 * c)
                for j, sel in enumerate((hot[:, 0], swap[:, :])):
                    nc.gpsimd.tensor_tensor(
                        masked[:, j].rearrange("p n (e r) -> p (n e) r", r=R),
                        xa[:, par].rearrange("p n (e r) -> p (n e) r", r=R),
                        sel.rearrange("p n e -> p (n e)").unsqueeze(2).to_broadcast([P, CT * E, R]),
                        ALU.mult).then_inc(mask_ready, 1)

            def hidden(c, fs):
                for f in fs:
                    wait(pool, in2_used, c * NF + f + 1)
                    if f == 0:
                        wait(pool, y_ready, c)
                    nc.gpsimd.tensor_tensor(hid[:, f], relu[:, f % 2, 0], relu[:, f % 2, 1],
                                            ALU.add).then_inc(hid_ready, 1)

            norms.wait_weights(pool)
            norm(0, 0)
            norm(1, 1)
            norms.blank_values(pool)
            mask(0, 0)

            def body(c, par):
                if not beyond(c + 2):
                    norm(c + 2, par)
                hidden(c, range(NF // 2))
                if not beyond(c + 1):
                    mask(c + 1, 1 - par)
                hidden(c, range(NF // 2, NF))
                residual(c)
            chunks(body, pool, 2)
            steps.stage_values(pool, 0, 0)
            steps.stage_values(pool, 0, 1)
            steps.part_maxima(pool, 0, 0)

        @block.tensor
        def _(pe):
            def turn_x(c, par):
                pe.wait_ge(xn_ready, c + 1)
                wait(pe, xt_copied, c)
                wait(pe, vx_copied, (c - 1) * CT + 3)
                for n in range(CT):
                    last = nc.tensor.transpose(psum[:, 0, n * P:(n + 1) * P], xn[:, par, n], ident[:, :])
                last.then_inc(xt_ready, 1)

            def products(c, par):
                pe.wait_ge(xt_copied, c + 1)
                for j, w in enumerate((wq, wk)):
                    wait(pe, qk_copied, 2 * c + j - 1)
                    nc.tensor.matmul(psum[:, 1 + j, :], w[:, :], xnT[:, par], start=True, stop=True).then_inc(qk_ready, 1)
                if not (isinstance(c, int) and c < 2):
                    pe.wait_ge(mt_copied, 2 * c)
                for n in range(CT):
                    if n != 2:
                        wait(pe, vx_copied, c * CT + n // 3)
                    nc.tensor.matmul(psum[:, VX_BANKS[n], 0:XW], xnT[:, par, n * P:(n + 1) * P], wx[:, :],
                                     start=True, stop=True).then_inc(vx_ready, 1)

            def turn_masked(c):
                if isinstance(c, int) and c == 0:
                    pe.wait_ge(vx_copied, 2 * CT)
                for j in range(2):
                    pe.wait_ge(mask_ready, 2 * c + j + 1)
                    for n in range(CT):
                        last = nc.tensor.transpose(psum[:, 3 + j, n * P:(n + 1) * P], masked[:, j, n], ident[:, :])
                    last.then_inc(mt_ready, 1)

            halves = iter(FIRST_HALVES)

            taken = {c: iter(plan) for c, plan in EARLY_HALVES.items()}

            def maxima(c):
                if early(c):
                    for _ in range(next(taken[c])):
                        steps.first_half(pe, *next(halves), 0)

            def hidden(c, par):
                pe.wait_ge(mt_copied, 2 * c + 2)
                if isinstance(c, int) and c == CHUNKS - 2:
                    pe.wait_ge(vx_copied, CT * CHUNKS)
                    pe.wait_ge(qk_copied, 2 * CHUNKS)

                def first_expert(f):
                    wait(pe, in2_used, c * NF + f - 1)
                    fs = slice(f * P, (f + 1) * P)
                    nc.tensor.matmul(psum[:, 6 + f % 2, :], wi[:, fs], xnT[:, par], start=True, stop=False)
                    maxima(c)
                    nc.tensor.matmul(psum[:, 6 + f % 2, :], wb[:, fs], maskedT[:, 0], start=False,
                                     stop=True).then_inc(in_ready, 1)
                    maxima(c)

                def second_expert(f):
                    pe.wait_ge(in1_used, c * NF + f + 1)
                    fs = slice(f * P, (f + 1) * P)
                    nc.tensor.matmul(psum[:, 6 + f % 2, :], wb[:, fs], maskedT[:, 1], start=False, stop=True,
                                     skip_group_check=True).then_inc(in_ready, 1)
                    maxima(c)

                for f in range(0, NF, 2):
                    first_expert(f)
                    first_expert(f + 1)
                    second_expert(f)
                    second_expert(f + 1)

            def output(c):
                wait(pe, y_chain, 2 * c - 1)
                pe.wait_ge(hid_ready, (c + 1) * NF)
                for n in range(CT):
                    for f in range(NF):
                        last = nc.tensor.matmul(psum[:, 5, n * P:(n + 1) * P], hid[:, f, n * P:(n + 1) * P],
                                                wo[:, f], start=(f == 0), stop=(f == NF - 1))
                    maxima(c)
                last.then_inc(y_ready, 1)

            norms.wait_weights(pe)
            for c in range(2):
                turn_x(c, c)
                products(c, c)
            turn_masked(0)

            def body(c, par):
                hidden(c, par)
                if not beyond(c + 2):
                    turn_x(c + 2, par)
                if not beyond(c + 1):
                    turn_masked(c + 1)
                if not beyond(c + 2):
                    products(c + 2, par)
                maxima(c)
                output(c)
            chunks(body, pe, 2)
            norms.wait_constants(pe)
            steps.turn_maxima(pe, 0, 0, 2)

        @block.scalar
        def _(act):
            def copy_x(c, par):
                act.wait_ge(xt_ready, c + 1)
                wait(act, in_ready, 2 * NF * (c - 1))
                nc.scalar.activation(xnT[:, par], psum[:, 0, :], ACT.Copy).then_inc(xt_copied, 1)

            def copy_qk(c, par):
                for j, (bias, scale) in enumerate(((bqs[:, :], SCALE), (bcol[:, BK:BK + 1], 1.0))):
                    act.wait_ge(qk_ready, 2 * c + j + 1)
                    wait(act, split, 10 * (c - 1) - 5 * (1 - j))
                    nc.scalar.activation(proj[:, par, j], psum[:, 1 + j, :], ACT.Identity, bias=bias,
                                         scale=scale).then_inc(qk_copied, 1)

            def gate(c):
                act.wait_ge(pick, c * PICK + SHIFTED)
                nc.scalar.activation(expd[:, :, :], shifted[:, :, :], ACT.Exp).then_inc(exps, 1)
                nc.scalar.activation(egap[:, :], gap[:, :], ACT.Exp).then_inc(exps, 1)

            def copy_masked(c):
                wait(act, in_ready, 2 * NF * c)
                for j in range(2):
                    act.wait_ge(mt_ready, 2 * c + j + 1)
                    nc.scalar.activation(maskedT[:, j], psum[:, 3 + j, :], ACT.Copy).then_inc(mt_copied, 1)

            def body(c, par):
                for f in range(0, NF, 2):
                    for k in range(2):
                        act.wait_ge(in_ready, 2 * (c * NF + f) + k + 1)
                        wait(act, hid_ready, c * NF + f + k - 1)
                        nc.scalar.activation(relu[:, k, 0], psum[:, 6 + k, :], ACT.Relu,
                                             bias=bcol[:, BI + f + k:BI + f + k + 1]).then_inc(in1_used, 1)
                    for k in range(2):
                        act.wait_ge(in_ready, 2 * (c * NF + f) + k + 3)
                        nc.scalar.activation(relu[:, k, 1], psum[:, 6 + k, :], ACT.Relu,
                                             bias=bcol[:, BI + f + k:BI + f + k + 1]).then_inc(in2_used, 1)
                    if f == 0 and not beyond(c + 1):
                        gate(c + 1)
                if not beyond(c + 2):
                    copy_x(c + 2, par)
                if not beyond(c + 1):
                    copy_masked(c + 1)
                if not beyond(c + 2):
                    copy_qk(c + 2, par)

            copy_x(0, 0)
            norms.square(act, 1)
            norms.wait_constants(act)
            copy_qk(0, 0)
            norms.square(act, 2)
            copy_x(1, 1)
            norms.square(act, 3)
            norms.root_of(act, 1)
            copy_masked(0)
            gate(0)
            copy_qk(1, 1)
            chunks(body, act, 2)
            steps.copy_maxima(act, 0, 0, 2)

        @block.vector
        def _(dve):
            def copy_products(c, par):
                for n in range(CT):
                    dve.wait_ge(vx_ready, c * CT + n + 1)
                    bank = psum[:, VX_BANKS[n]]
                    nc.vector.tensor_tensor(
                        values[:, bass.ds((c // 2) * PAIRS, PAIRS), bass.ds((c % 2) * CT + n, 1)].rearrange(
                            "p u o a d -> p (u o) (a d)"),
                        bank[:, XV:XV + C].rearrange("p (u w) -> p u w", u=PAIRS),
                        brow[:, BV:BV + C].rearrange("p (u w) -> p u w", u=PAIRS), ALU.add)
                    nc.vector.tensor_tensor(logit[:, par, n], bank[:, XG:XG + E], brow[:, GB:GB + E], ALU.add)
                    if n == 0:
                        wait(dve, mask_ready, 2 * c - 2)
                    nc.vector.tensor_copy(xa[:, par, n], bank[:, XA:XA + C]).then_inc(vx_copied, 1)

            def split_qk(c, par):
                for j in range(2):
                    dve.wait_ge(qk_copied, 2 * c + j + 1)
                    k0 = 2 * 5 * c + 5 * j
                    wait(dve, parts_out[j], 16 * NC * c)
                    nc.vector.tensor_copy(parts[:, j, 0], proj[:, par, j]).then_inc(split, 1)
                    dve.wait_ge(split, k0 + 1)
                    nc.vector.tensor_tensor(res[:, j, 0], proj[:, par, j], parts[:, j, 0], ALU.subtract).then_inc(split, 1)
                    dve.wait_ge(split, k0 + 2)
                    nc.vector.tensor_copy(parts[:, j, 1], res[:, j, 0]).then_inc(split, 1)
                    dve.wait_ge(split, k0 + 3)
                    nc.vector.tensor_tensor(res[:, j, 1], res[:, j, 0], parts[:, j, 1], ALU.subtract).then_inc(split, 1)
                    dve.wait_ge(split, k0 + 4)
                    nc.vector.tensor_copy(parts[:, j, 2], res[:, j, 1]).then_inc(split, 1)

            def wide(a):
                return a.unsqueeze(2).to_broadcast([P, CT, E])

            def linker(c, step):
                def link(ins):
                    ins.then_inc(pick, 1)
                    step[0] += 1
                    dve.wait_ge(pick, c * PICK + step[0])
                return link

            def choose(c, par):
                step = [0]
                link = linker(c, step)

                wait(dve, mask_ready, 2 * c)
                dve.wait_ge(vx_copied, CT * (c + 1))
                link(nc.vector.tensor_reduce(top[:, 0], logit[:, par], AX_X, ALU.max))
                source = logit[:, par]
                for j in range(2):
                    link(nc.vector.tensor_tensor(below[:, :, :], source, wide(top[:, j]), ALU.is_lt))
                    link(nc.vector.scalar_tensor_tensor(
                        cand[:, :, :].rearrange("p n e -> p (n e)"), below[:, :, :].rearrange("p n e -> p (n e)"),
                        float(E), iota[:, :, :].rearrange("p n e -> p (n e)"), ALU.mult, ALU.add))
                    link(nc.vector.tensor_reduce(first[:, j], cand[:, :, :], AX_X, ALU.min))
                    link(nc.vector.tensor_tensor(hot[:, j], iota[:, :, :], wide(first[:, j]), ALU.is_equal))
                    if j == 0:
                        link(nc.vector.scalar_tensor_tensor(
                            rest[:, :, :].rearrange("p n e -> p (n e)"), hot[:, 0].rearrange("p n e -> p (n e)"),
                            -3e38, logit[:, par].rearrange("p n e -> p (n e)"), ALU.mult, ALU.add))
                        link(nc.vector.tensor_reduce(top[:, 1], rest[:, :, :], AX_X, ALU.max))
                        source = rest[:, :, :]
                link(nc.vector.tensor_tensor(swap[:, :, :], hot[:, 1], hot[:, 0], ALU.subtract))
                assert step[0] == SWAPPED
                link(nc.vector.tensor_tensor(shifted[:, :, :], logit[:, par], wide(top[:, 0]), ALU.subtract))
                link(nc.vector.tensor_tensor(gap[:, :], top[:, 1], top[:, 0], ALU.subtract))
                assert step[0] == SHIFTED

            def gate_sum(c, par):
                step = [SHIFTED]
                link = linker(c, step)
                dve.wait_ge(exps, 2 * c + 2)
                wait(dve, y_chain, 2 * (c - 1))
                link(nc.vector.tensor_reduce(esum[:, :], expd[:, :, :], AX_X, ALU.add))
                link(nc.vector.reciprocal(einv[:, :], esum[:, :]))
                link(nc.vector.tensor_scalar(etop[:, :], egap[:, :], 1.0, None, ALU.add))
                link(nc.vector.tensor_tensor(vsum[:, par], etop[:, :], einv[:, :], ALU.mult))
                assert step[0] == PICK

            def add_output(c, par):
                wait(dve, y_chain, 2 * c)
                dve.wait_ge(y_ready, c + 1)
                nc.vector.tensor_tensor(outb[:, :, :], psum[:, 5, :].rearrange("p (n d) -> p n d", n=CT),
                                        bo2[:, :].unsqueeze(1).to_broadcast([P, CT, C]), ALU.add).then_inc(y_chain, 1)
                dve.wait_ge(y_chain, 2 * c + 1)
                dve.wait_ge(res_ready, c + 1)
                for n in range(CT):
                    tile = acc[:, bass.ds(c * CT + n, 1), :].rearrange("p o d -> p (o d)")
                    last = nc.vector.scalar_tensor_tensor(tile, outb[:, n], vsum[:, par, n:n + 1], tile,
                                                          ALU.mult, ALU.add)
                last.then_inc(y_chain, 1)

            norms.centre(dve, 1)
            norms.make_constants(dve)
            norms.wait_constants(dve)
            for b in range(2, B):
                norms.centre(dve, b)
            copy_products(0, 0)
            choose(0, 0)
            norms.variance(dve, 1)
            copy_products(1, 1)
            norms.refine(dve, 1)
            split_qk(0, 0)
            gate_sum(0, 0)
            choose(1, 1)
            split_qk(1, 1)

            halves = iter(FIRST_HALVES)

            def body(c, par):
                if early(c):
                    for _ in range(sum(EARLY_HALVES[c])):
                        half = next(halves)
                        steps.reduce_half(dve, 0, *half, half[-1])
                if not beyond(c + 1):
                    gate_sum(c + 1, 1 - par)
                if not beyond(c + 2):
                    copy_products(c + 2, par)
                    choose(c + 2, par)
                    split_qk(c + 2, par)
                add_output(c, par)
            chunks(body, dve, 2)
            dve.wait_ge(y_chain, 2 * CHUNKS)

        @block.sync
        def _(sp):
            def store(c):
                for j, (dst, combos) in enumerate(((q_parts, COMBOS_Q), (k_parts, COMBOS_K))):
                    view = dst.rearrange("(b u) a c d t -> b c (u a) d t", b=B)
                    sp.wait_ge(split, 10 * c + 5 * j + 5)
                    for m, part in enumerate(combos):
                        sp.dma_start(
                            view[bass.ds(c // 2, 1), m, :, :, bass.ds((c % 2) * CHUNK, CHUNK)].rearrange(
                                "o g d t -> (o g) d t"),
                            parts[:, j, part]).then_inc(parts_out[j], 16)
            steps.stage_fixed(sp)
            first = NT // CT
            for c in range(first):
                store(c)
            for j in range(2):
                sp.wait_ge(parts_out[j], 16 * NC * first)
            steps.stage(sp, 0, 0)
            steps.stage(sp, 0, 1)
            with sp.Fori(0, CHUNKS - first) as c:
                store(c + first)
            for j in range(2):
                sp.wait_ge(parts_out[j], 16 * NC * CHUNKS)
            steps.stage_maxima(sp, 0, 0)


def phase2(nc, sem, psum, values, heads_out, ident, ident_b, k_stage, q_stage, v_stage, factor,
           acc, wp, out, steps):
    with ExitStack() as ph:
        def tmp(name, shape, dt=F32):
            return ph.enter_context(nc.sbuf_tensor(name, shape, dt))

        probs = tmp("probs", [P, PROBS, 2, CHUNK])
        y_cols = tmp("y_cols", [P, CHUNK])
        y_turned = tmp("y_turned", [P, CT, 4, D + 1])
        y_inv = tmp("y_inv", [P, CT, 4])
        turned = tmp("turned", [P, 2, CHUNK])

        s_ready = sem("scores_in_psum")
        e_ready = sem("exponentials")
        d_ready = sem("diagonal_done")
        m_staged, v_staged, mt_copied = steps.m_staged, steps.v_staged, steps.mt_copied
        pv_done, yt_copied = steps.pv_done, steps.yt_copied
        y_done = sem("y_normalised")
        y_copied = sem("y_copied")
        yt_ready = sem("y_t_in_psum")
        y_inverse = sem("y_inverse")
        turn_ready = sem("heads_t_in_psum")
        turn_copied = sem("heads_t_copied")
        last_copied = sem("last_heads_t_copied")
        out_ready = sem("projection_in_psum")
        out_added = sem("projection_added")
        stored = sem("output_stored")
        EARLY = CHUNKS - NT // CT
        TURN_BANK = [4] * (EARLY + 1) + [0]
        OUT_BANK = [5] * (EARLY + 1) + [1]

        TILE_STEPS = 2 * NT
        y_ps = psum[:, 6]
        IN_TURN = (7, 4, 5)
        TURNS = HALVES + 2
        Y_STEP, MAX_STEP = 4, 6
        Y_TURN, M_TURN = 4 * (Y_STEP + 1), 4 * (MAX_STEP + 1) + 1
        LAST_TURN = (UNITS - 1 + Y_TURN) % len(IN_TURN)

        def bank_of(v, turn):
            return IN_TURN[(v + turn) % len(IN_TURN)]

        def half_turn(i, k):
            n = 4 * i + k
            return n + (n >= Y_TURN) + (n + 1 >= M_TURN)

        def half_of(t, v, i, k):
            j, h = 2 * (i % CT) + k // 2, k % 2
            if i < CT:
                return None if beyond(t, v + 1) else (t, v + 1, 1, j, h)
            return None if beyond(t, v + 2) else (t, v + 2, 0, j, h)

        def beyond(t, v):
            return isinstance(t, int) and v >= UNITS

        def final(t, v):
            return isinstance(t, int) and v == UNITS - 1

        def units(body, eng):
            body(0, 0)
            body(0, 1)
            with eng.Fori(0, (UNITS - 5) // RING) as t:
                for v in range(2, RING + 2):
                    body(t, v)
            for v in range(UNITS - 3, UNITS):
                body(0, v)

        def norm_y(eng, tensor_tensor, t, v):
            u = number(t, v)
            eng.wait_ge(y_inverse, u + 1)
            for a in range(2):
                tensor_tensor(
                    heads_out[:, :, bass.ds(u * 2 * D + a * D, D)].rearrange("p (c q) d -> p c q d", c=2),
                    y_turned[:, :, 2 * a:2 * a + 2, 0:D].rearrange("p q c d -> p c q d"),
                    y_inv[:, :, 2 * a:2 * a + 2].rearrange("p q c -> p c q").unsqueeze(3).to_broadcast(
                        [P, 2, CT, D]), ALU.mult).then_inc(y_done, 1)

        with nc.Block() as block:
            @block.sync
            def _(sp):
                def body(t, v):
                    if not beyond(t, v + 2):
                        steps.stage(sp, t, v + 2)
                    if not beyond(t, v + 1):
                        steps.stage_maxima(sp, t, v + 1)
                units(body, sp)
                for c in range(CHUNKS):
                    sp.wait_ge(out_added, c + 1)
                    sp.dma_start(out.rearrange("b (n p) d -> p (b n) d", p=P)[:, c * CT:(c + 1) * CT, :],
                                 acc[:, c * CT:(c + 1) * CT, :]).then_inc(stored, 16)
                sp.wait_ge(stored, 16 * CHUNKS)

            @block.gpsimd
            def _(pool):
                def body(t, v):
                    u, slot = number(t, v), slot_of(v)
                    for i in range(NT):
                        c = i // CT
                        wait(pool, e_ready, u * TILE_STEPS + 2 * i + c + 1)
                        tile = probs[:, (2 * i + c) % PROBS, :, (i % CT) * P:(i % CT + 1) * P]
                        nc.gpsimd.tensor_tensor(tile, tile, factor[:, slot], ALU.mult).then_inc(d_ready, 1)
                        if i == 1 and not beyond(t, v + 2):
                            steps.stage_values(pool, t, v + 2)
                        if i == NT // 2 and not beyond(t, v + 1):
                            steps.part_maxima(pool, t, v + 1)
                        if i == 5 and not (isinstance(t, int) and v == 0):
                            norm_y(pool, nc.gpsimd.tensor_tensor, t, v - 1)
                units(body, pool)

            @block.tensor
            def _(pe):
                def scores(t, v, i, c, a):
                    u, slot = number(t, v), slot_of(v)
                    n = 2 * i + c
                    if n == 0 and a == 0:
                        pe.wait_ge(m_staged[slot], fill(t, v) * 16)
                    if a == 0:
                        wait(pe, e_ready, u * TILE_STEPS + n - 1)
                    for t0, t1, form, rows in regions_by_queries(i, c):
                        ins = nc.tensor.matmul(
                            psum[:, 2 * c + a, t0 - c * 512:t1 - c * 512],
                            k_stage[0:rows, slot, a, form, i * P:(i + 1) * P],
                            q_stage[0:rows, slot, t0:t1], start=True, stop=True)
                    if a == 1:
                        ins.then_inc(s_ready, 1)

                def weigh(t, v, i):
                    u, slot = number(t, v), slot_of(v)
                    if i == 0:
                        pe.wait_ge(v_staged, u + 1)
                        wait(pe, y_copied, u)
                    pe.wait_ge(e_ready, u * TILE_STEPS + 2 * i + 2)
                    pe.wait_ge(d_ready, u * NT + i + 1)
                    for a in range(2):
                        for c in range(2):
                            g = 32 * (2 * a + c)
                            ins = nc.tensor.matmul(y_ps[g:g + VP, :], v_stage[:, slot, i, a, :],
                                                   probs[:, (2 * i + c) % PROBS, a, :],
                                                   start=(i == 0), stop=(i == NT - 1))
                    ins.then_inc(pv_done, 1)

                def wait_turn(t, v, turn):
                    u = number(t, v)
                    halves = turn - (turn > Y_TURN) - (turn > M_TURN)
                    prev, pu = turn - len(IN_TURN), u
                    if prev < 0:
                        prev, pu = prev + TURNS, u - 1
                    last = isinstance(u, int) and pu * TURNS + prev >= (UNITS - 2) * TURNS + half_turn(CT, 0)
                    if isinstance(u, int) and (last or pu < 0 or (pu == 0 and prev == Y_TURN)):
                        wait(pe, steps.half_used, min(UNITS * HALVES, HALVES * (u + 1) + 16 + max(halves - 2, 0)))
                        wait(pe, yt_copied, u if turn > Y_TURN else u - 1)
                        wait(pe, mt_copied, min(UNITS, u + 2 if turn > M_TURN else u + 1))
                    elif prev == Y_TURN:
                        wait(pe, yt_copied, pu)
                    elif prev == M_TURN:
                        wait(pe, mt_copied, pu + 2)
                    else:
                        n = prev - (prev > Y_TURN) - (prev > M_TURN)
                        wait(pe, steps.half_used, HALVES * (pu + 1) + 16 + n + 1)

                def turn_y(t, v, bank):
                    u = number(t, v)
                    pe.wait_ge(y_copied, u + 1)
                    for q in range(CT):
                        ins = nc.tensor.transpose(psum[:, bank, q * P:(q + 1) * P], y_cols[:, q * P:(q + 1) * P],
                                                  ident[:, :])
                    ins.then_inc(yt_ready, 1)

                def turn_heads(c):
                    batch = c * CT // NT
                    pe.wait_ge(y_done, 2 * PAIRS * (batch + 1))
                    wait(pe, turn_copied, min(c, EARLY))
                    if c == 0:
                        pe.wait_ge(steps.half_used, UNITS * HALVES)
                        pe.wait_ge(mt_copied, UNITS)
                        pe.wait_ge(yt_copied, UNITS - 2)
                    for n in range(CT):
                        ins = nc.tensor.transpose(psum[:, TURN_BANK[c], n * P:(n + 1) * P],
                                                  heads_out[:, c * CT % NT + n, batch * C:(batch + 1) * C],
                                                  ident[:, :])
                    ins.then_inc(turn_ready, 1)

                def project(c):
                    if c == CHUNKS - 1:
                        pe.wait_ge(last_copied, 1)
                    else:
                        pe.wait_ge(turn_copied, c + 1)
                    wait(pe, out_added, min(c, EARLY))
                    for n in range(CT):
                        ins = nc.tensor.matmul(psum[:, OUT_BANK[c], n * P:(n + 1) * P],
                                               turned[:, c % 2, n * P:(n + 1) * P], wp[:, :], start=True, stop=True)
                    ins.then_inc(out_ready, 1)

                for half in FIRST_HALVES[EARLY_SUM:]:
                    steps.first_half(pe, *half, 4)

                def body(t, v):
                    start = isinstance(t, int) and v == 0
                    for i in range(NT):
                        def max_part(k):
                            half = half_of(t, v, i, k)
                            if half is not None:
                                wait_turn(t, v, half_turn(i, k))
                                steps.max_half(pe, *half, bank_of(v, half_turn(i, k)))

                        max_part(0)
                        if i >= LAG:
                            weigh(t, v, i - LAG)
                        elif not start:
                            weigh(t, v - 1, NT + i - LAG)
                        max_part(1)
                        scores(t, v, i, 0, 0)
                        scores(t, v, i, 0, 1)
                        max_part(2)
                        scores(t, v, i, 1, 0)
                        scores(t, v, i, 1, 1)
                        max_part(3)
                        if i == Y_STEP and not start:
                            wait_turn(t, v, Y_TURN)
                            turn_y(t, v - 1, bank_of(v, Y_TURN))
                        if i == MAX_STEP and not beyond(t, v + 1):
                            wait_turn(t, v, M_TURN)
                            steps.turn_maxima(pe, t, v + 1, bank_of(v, M_TURN))
                        if final(t, v):
                            if 1 <= i <= EARLY:
                                project(i - 1)
                            if i < EARLY:
                                turn_heads(i)
                units(body, pe)
                for i in range(NT - LAG, NT):
                    weigh(0, UNITS - 1, i)
                pe.wait_ge(yt_copied, UNITS - 1)
                turn_y(0, UNITS - 1, IN_TURN[LAST_TURN])
                turn_heads(EARLY)
                turn_heads(EARLY + 1)
                project(EARLY)
                project(EARLY + 1)

            @block.scalar
            def _(act):
                def copy_y(t, v):
                    u = number(t, v)
                    act.wait_ge(pv_done, (u + 1) * NT)
                    wait(act, yt_ready, u)
                    nc.scalar.activation(y_cols[:, :], y_ps, ACT.Copy).then_inc(y_copied, 1)

                def copy_yt(t, v, bank):
                    u = number(t, v)
                    act.wait_ge(yt_ready, u + 1)
                    wait(act, y_done, 2 * u)
                    nc.scalar.activation(y_turned[:, :, :, :].rearrange("p q g w -> p (q g) w"),
                                         psum[:, bank].rearrange("p (g w) -> p g w", w=VP)[:, :, 0:D + 1],
                                         ACT.Copy).then_inc(yt_copied, 1)

                def body(t, v):
                    u = number(t, v)
                    for i in range(NT):
                        for c in range(2):
                            n = 2 * i + c
                            act.wait_ge(s_ready, u * TILE_STEPS + n + 1)
                            wait(act, pv_done, u * NT + i + 1 - PROBS // 2)
                            nc.scalar.activation(
                                probs[:, n % PROBS], psum[:, 2 * c:2 * c + 2, :], ACT.Exp).then_inc(e_ready, 1)
                            if n == 1 and not (isinstance(t, int) and v == 0):
                                copy_y(t, v - 1)
                        if i == Y_STEP and not (isinstance(t, int) and v == 0):
                            copy_yt(t, v - 1, bank_of(v, Y_TURN))
                        if i == MAX_STEP and not beyond(t, v + 1):
                            steps.copy_maxima(act, t, v + 1, bank_of(v, M_TURN))
                units(body, act)
                copy_y(0, UNITS - 1)
                copy_yt(0, UNITS - 1, IN_TURN[LAST_TURN])
                act.wait_ge(turn_ready, EARLY + 1)
                nc.scalar.activation(turned[:, EARLY % 2], psum[:, TURN_BANK[EARLY]], ACT.Copy).then_inc(turn_copied, 1)

            @block.vector
            def _(dve):
                def invert_sums(t, v):
                    u = number(t, v)
                    wait(dve, y_done, 2 * u)
                    dve.wait_ge(yt_copied, u + 1)
                    nc.vector.reciprocal(y_inv[:, :, :], y_turned[:, :, :, D]).then_inc(y_inverse, 1)

                def copy_turned(c):
                    dve.wait_ge(turn_ready, c + 1)
                    wait(dve, out_ready, c - 1)
                    nc.vector.tensor_copy(turned[:, c % 2], psum[:, TURN_BANK[c]]).then_inc(
                        last_copied if c == CHUNKS - 1 else turn_copied, 1)

                def add_projection(c):
                    dve.wait_ge(out_ready, c + 1)
                    tiles = acc[:, c * CT:(c + 1) * CT, :].rearrange("p n d -> p (n d)")
                    nc.vector.tensor_tensor(tiles, psum[:, OUT_BANK[c]], tiles, ALU.add).then_inc(out_added, 1)

                for half in FIRST_HALVES[EARLY_SUM:]:
                    steps.reduce_half(dve, 0, *half, 4 + half[-1])

                def body(t, v):
                    for i in range(NT):
                        for k in range(4):
                            if half_of(t, v, i, k) is not None:
                                steps.reduce_half(dve, *half_of(t, v, i, k), bank_of(v, half_turn(i, k)))
                        if i == 5 and not (isinstance(t, int) and v == 0):
                            invert_sums(t, v - 1)
                        if final(t, v):
                            if 1 <= i <= EARLY:
                                add_projection(i - 1)
                            if i < EARLY:
                                copy_turned(i)
                units(body, dve)
                invert_sums(0, UNITS - 1)
                norm_y(dve, nc.vector.tensor_tensor, 0, UNITS - 1)
                copy_turned(EARLY + 1)
                add_projection(EARLY)
                add_projection(EARLY + 1)


def regions_by_keys(j, h):
    lo, hi = h * 512, h * 512 + 512
    spans = ((0, j * P, 1, ALL), (j * P, (j + 1) * P, 0, ALL), ((j + 1) * P, T, 0, MAIN))
    return [(max(lo, s0), min(hi, s1), form, rows) for s0, s1, form, rows in spans if max(lo, s0) < min(hi, s1)]


def regions_by_queries(i, c):
    lo, hi = c * 512, c * 512 + 512
    spans = ((0, i * P, 0, MAIN), (i * P, (i + 1) * P, 0, ALL), ((i + 1) * P, T, 1, ALL))
    return [(max(lo, t0), min(hi, t1), form, rows) for t0, t1, form, rows in spans if max(lo, t0) < min(hi, t1)]


def rounded(v):
    bits = np.asarray(v, np.float32).view(np.uint32)
    return ((bits + 0x7FFF + ((bits >> 16) & 1)) & 0xFFFF0000).astype(np.uint32).view(np.float32)


def constants():
    def parts3(v):
        v = np.asarray(v, np.float32)
        a = rounded(v)
        b = rounded(v - a)
        return a, b, rounded(v - a - b)

    def bits(v):
        return (rounded(v).view(np.uint32) >> 16).astype(np.uint16)

    start = 2.0 ** (-2.0 ** (-(np.log2(H) - 3)))
    slopes = np.array([start * start ** i for i in range(H)]).astype(np.float32)
    pos = np.arange(T)
    lane = pos % P
    steps = range(1, P // STEP)
    q_rows = np.zeros((BR, T), np.float32)
    for m in steps:
        q_rows[m - 1] = lane >= m * STEP
    q_rows[3:6] = 1.0
    q_rows[6:9] = lane
    q_rows[9:12] = (pos // P - NT // 2) * P
    k_rows = np.zeros((H, BR, 2, T), np.float32)
    factors = np.zeros((P, H, P), np.float32)
    s_l, t_l = np.arange(P)[:, None], np.arange(P)[None, :]
    for h in range(H):
        step = rounded(slopes[h:h + 1] * np.float32(STEP))[0]
        for m in steps:
            k_rows[h, m - 1, 0] = np.where(lane < m * STEP, -step, 0.0)
        k_rows[h, 3:6, 1] = parts3(slopes[h] * (pos - T // 2).astype(np.float32))
        for p, part in enumerate(parts3(slopes[h:h + 1])):
            k_rows[h, 6 + p, 1] = -part[0]
            k_rows[h, 9 + p, 1] = -part[0]
        stairs = sum(((s_l < m * STEP) & (t_l >= m * STEP)).astype(np.float64) for m in steps)
        factors[:, h] = np.exp(float(slopes[h]) * np.minimum(s_l - t_l, 0) + float(step) * stairs)
    const_rows = np.stack([np.ones((2 * MX, T), np.float32), np.zeros((2 * MX, T), np.float32)])
    return dict(ident_in=np.eye(P, dtype=np.float32),
                iota_in=np.ascontiguousarray(np.broadcast_to(np.arange(E, dtype=np.float32), (P, CT, E))),
                q_rows=bits(q_rows), k_rows=bits(k_rows).reshape(PAIRS, 2, BR, 2, T),
                const_rows=bits(const_rows),
                factors=factors.reshape(P, PAIRS, 2, P).transpose(1, 0, 2, 3))


def kernel(L0_attn_x, L0_attn_W_qkv, L0_attn_b_qkv, L0_attn_W_proj, L0_attn_b_proj, L0_ffn_wi, L0_ffn_bi,
           L0_ffn_wo, L0_ffn_bo, L0_ffn_lora_A, L0_ffn_lora_B, L0_ffn_gate_w, L0_ffn_gate_b):
    import concourse.bacc as _bacc
    from concourse.bass_utils import run_bass_kernel_spmd as _run

    w_qkv, b_qkv = np.asarray(L0_attn_W_qkv), np.asarray(L0_attn_b_qkv)
    row = np.concatenate([b_qkv[2 * C:], np.asarray(L0_attn_b_proj), np.asarray(L0_ffn_bo),
                          np.asarray(L0_ffn_gate_b)])
    laid = dict(
        x=np.asarray(L0_attn_x),
        w_q=w_qkv[:, 0:C], w_k=w_qkv[:, C:2 * C],
        w_x=np.concatenate([w_qkv[:, 2 * C:], np.asarray(L0_ffn_lora_A).reshape(E * R, C).T,
                            np.asarray(L0_ffn_gate_w).T], axis=1),
        w_i=np.asarray(L0_ffn_wi).T,
        w_b=np.asarray(L0_ffn_lora_B).transpose(0, 2, 1).reshape(E * R, F),
        w_o=np.asarray(L0_ffn_wo).T.reshape(F // P, P, C).transpose(1, 0, 2),
        w_p=np.asarray(L0_attn_W_proj),
        bias_rows=np.broadcast_to(row, (P, row.shape[0])),
        bias_cols=np.concatenate([b_qkv[0:2 * C].reshape(2, C).T, np.asarray(L0_ffn_bi).reshape(F // P, P).T], axis=1),
    )
    laid.update(constants())
    nc = _bacc.Bacc("TRN2", target_bir_lowering=False, num_devices=1)
    arrays, args = {}, {}
    for name, a in laid.items():
        a = np.ascontiguousarray(a)
        arrays[f"in_{name}"] = a
        args[name] = nc.dram_tensor(f"in_{name}", a.shape, mybir.dt.from_np(a.dtype), kind="ExternalInput").ap()
    args["out"] = nc.dram_tensor("out", (B, T, C), F32, kind="ExternalOutput").ap()
    build(nc, **args)
    r = _run(nc, [arrays], core_ids=[0])
    return r.results[0]["out"]
```
